# Optimizing a Trainium2 kernel written in Bass

```python
import numpy as np
import jax
import jax.numpy as jnp

def _softmax(x, axis=-1):
    return jax.nn.softmax(x, axis=axis)

def _gelu(x):
    return jax.nn.gelu(x, approximate=True)

def _silu(x):
    return jax.nn.silu(x)

def _sigmoid(x):
    return jax.nn.sigmoid(x)

def _layernorm(x, axis=-1, eps=1e-05):
    m = jnp.mean(x, axis=axis, keepdims=True)
    v = jnp.var(x, axis=axis, keepdims=True)
    return (x - m) / jnp.sqrt(v + eps)

def _scatter_add(tgt, idx, src, axis=0):
    return tgt.at[idx].add(src)

def _segment_sum(src, seg, n):
    return jax.ops.segment_sum(src, seg, n)
kernel_name = 'mk_xattn_ffn_d1_seqx_r4_270d4d'

def setup_inputs(seed: int=0):
    np.random.seed(seed)
    _w = jnp.asarray

    def _rec_inputs():
        import jax
        import jax.numpy as jnp
        _rk = jax.random.key(seed)
        x = -0.0005207 + 1.001 * jax.random.normal(jax.random.fold_in(_rk, 1), (8, 256, 256), jnp.float32)
        _lenS = 256 - jax.random.randint(jax.random.fold_in(_rk, 7), (8,), 0, max(1, 256 // 4) + 1, jnp.int32)
        _lenS2 = 256 - jax.random.randint(jax.random.fold_in(_rk, 8), (8,), 0, max(1, 256 // 4) + 1, jnp.int32)
        _ctx_1024P = jax.random.normal(jax.random.fold_in(_rk, 11), (8, 16, 256), jnp.float32)
        _ctx_1024c = jax.random.dirichlet(jax.random.fold_in(_rk, 511), 0.3 * jnp.ones((16,), jnp.float32), (8, 256))
        _ctx_1024t = jnp.einsum('bsk,bkd->bsd', _ctx_1024c, _ctx_1024P)
        _ctx_1024t = _ctx_1024t * jax.lax.rsqrt(jnp.mean(jnp.square(_ctx_1024t)) + 1e-12) * 0.953939
        ctx_1024 = -0.000514642 + 1.00011 * (_ctx_1024t + 0.3 * jax.random.normal(jax.random.fold_in(_rk, 611), (8, 256, 256), jnp.float32))
        return (x, ctx_1024)
    x, ctx_1024 = _rec_inputs()

    def _L0_xattn_setup():
        import jax, jax.numpy as jnp
        import numpy as np
        DIM = 256
        HEADS = 8
        HEAD_DIM = DIM // HEADS
        TAU = HEAD_DIM ** 0.5
        BS, SEQ = (1, 512)
        key = jax.random.key(seed)
        kq, kk, kv, kb = jax.random.split(key, 4)
        q = jax.random.normal(kq, (BS, SEQ, DIM), jnp.float32)
        k = jax.random.normal(kk, (BS, SEQ, DIM), jnp.float32)
        v = jax.random.normal(kv, (BS, SEQ, DIM), jnp.float32)
        Wi_w = jnp.zeros((HEADS, 3 * DIM), jnp.float32)
        Wi_b = 0.1 * jax.random.normal(kb, (HEADS,), jnp.float32)
        Wf_w = jnp.zeros((HEADS, 3 * DIM), jnp.float32)
        Wf_b = jnp.linspace(3.0, 6.0, HEADS, dtype=jnp.float32)
        gn_w = jnp.ones((DIM,), jnp.float32)
        gn_b = jnp.zeros((DIM,), jnp.float32)
        return {'q': q, 'k': k, 'v': v, 'Wi_w': Wi_w, 'Wi_b': Wi_b, 'Wf_w': Wf_w, 'Wf_b': Wf_b, 'gn_w': gn_w, 'gn_b': gn_b}
    _L0_xattn_all = _L0_xattn_setup()
    _L0_xattn_in = {k: v for k, v in _L0_xattn_all.items() if k in ('Wi_w', 'Wi_b', 'Wf_w', 'Wf_b', 'gn_w', 'gn_b')}
    del _L0_xattn_all

    def _L0_ffn_setup():
        import jax, jax.numpy as jnp
        import numpy as np
        LN_EPS = 1e-05
        NORM_EPS = 1e-12

        def _layernorm(x, gamma, beta):
            mu = x.mean(axis=-1, keepdims=True)
            var = ((x - mu) ** 2).mean(axis=-1, keepdims=True)
            return (x - mu) * jax.lax.rsqrt(var + LN_EPS) * gamma + beta

        def _l2norm(x, axis):
            n = jnp.sqrt((x ** 2).sum(axis=axis, keepdims=True))
            return x / jnp.maximum(n, NORM_EPS)
        key = jax.random.key(seed)
        ks = jax.random.split(key, 4)
        B, N, D, E, S, H = (64, 64, 256, 16, 16, 64)
        x = jax.random.normal(ks[0], (B, N, D), dtype=jnp.float32)
        mu = jax.random.normal(ks[1], (D, E, S), dtype=jnp.float32) / np.sqrt(D)
        w1 = jax.random.normal(ks[2], (E, D, H), dtype=jnp.float32) * np.sqrt(2.0 / D)
        w2 = jax.random.normal(ks[3], (E, H, D), dtype=jnp.float32) * np.sqrt(2.0 / (H + D))
        return {'x': x, 'ln_gamma': jnp.ones((D,), jnp.float32), 'ln_beta': jnp.zeros((D,), jnp.float32), 'mu': mu, 'scale': jnp.ones((1,), jnp.float32), 'w1': w1, 'b1': jnp.zeros((E, H), jnp.float32), 'w2': w2, 'b2': jnp.zeros((E, D), jnp.float32)}
    _L0_ffn_all = _L0_ffn_setup()
    _L0_ffn_in = {k: v for k, v in _L0_ffn_all.items() if k in ('ln_gamma', 'ln_beta', 'mu', 'scale', 'w1', 'b1', 'w2', 'b2')}
    del _L0_ffn_all
    return {'x': x, 'ctx_1024': ctx_1024, 'L0_xattn_Wi_w': _L0_xattn_in['Wi_w'], 'L0_xattn_Wi_b': _L0_xattn_in['Wi_b'], 'L0_xattn_Wf_w': _L0_xattn_in['Wf_w'], 'L0_xattn_Wf_b': _L0_xattn_in['Wf_b'], 'L0_xattn_gn_w': _L0_xattn_in['gn_w'], 'L0_xattn_gn_b': _L0_xattn_in['gn_b'], 'L0_ffn_ln_gamma': _L0_ffn_in['ln_gamma'], 'L0_ffn_ln_beta': _L0_ffn_in['ln_beta'], 'L0_ffn_mu': _L0_ffn_in['mu'], 'L0_ffn_scale': _L0_ffn_in['scale'], 'L0_ffn_w1': _L0_ffn_in['w1'], 'L0_ffn_b1': _L0_ffn_in['b1'], 'L0_ffn_w2': _L0_ffn_in['w2'], 'L0_ffn_b2': _L0_ffn_in['b2']}

def reference(x, ctx_1024, L0_xattn_Wi_w, L0_xattn_Wi_b, L0_xattn_Wf_w, L0_xattn_Wf_b, L0_xattn_gn_w, L0_xattn_gn_b, L0_ffn_ln_gamma, L0_ffn_ln_beta, L0_ffn_mu, L0_ffn_scale, L0_ffn_w1, L0_ffn_b1, L0_ffn_w2, L0_ffn_b2):
    import jax
    import jax.numpy as jnp

    def _L0_xattn_ref(q, k, v, Wi_w, Wi_b, Wf_w, Wf_b, gn_w, gn_b):
        import jax, jax.numpy as jnp
        import numpy as np
        DIM = 256
        HEADS = 8
        HEAD_DIM = DIM // HEADS
        TAU = HEAD_DIM ** 0.5
        BS, SEQ = (1, 512)
        bs, seq, dim = q.shape
        gate_in = jnp.concatenate([q, k, v], axis=-1)
        itilde = jnp.einsum('bsd,hd->bhs', gate_in, Wi_w) + Wi_b[None, :, None]
        ftilde = jnp.einsum('bsd,hd->bhs', gate_in, Wf_w) + Wf_b[None, :, None]
        csum = jnp.cumsum(jax.nn.log_sigmoid(ftilde), axis=-1)
        Fmat = csum[..., :, None] - csum[..., None, :]
        mask = jnp.tril(jnp.ones((seq, seq), dtype=bool))
        F_act = jnp.where(mask, Fmat, -jnp.inf)
        Dtilde = F_act + itilde[..., None, :]
        max_d = jnp.max(Dtilde, axis=-1, keepdims=True)
        D = jnp.exp(Dtilde - max_d)
        qh = q.reshape(bs, seq, HEADS, HEAD_DIM).transpose(0, 2, 1, 3)
        kh = k.reshape(bs, seq, HEADS, HEAD_DIM).transpose(0, 2, 1, 3)
        vh = v.reshape(bs, seq, HEADS, HEAD_DIM).transpose(0, 2, 1, 3)
        Ctilde = jnp.einsum('bhid,bhjd->bhij', qh, kh) * D / TAU
        maxit = jnp.maximum(jnp.abs(jnp.sum(Ctilde, axis=-1, keepdims=True)), jnp.exp(-max_d))
        Htilde = jnp.einsum('bhij,bhjd->bhid', Ctilde, vh) / (maxit + 1e-06)
        x = Htilde.transpose(0, 2, 1, 3).reshape(bs * seq, HEADS, HEAD_DIM)
        mean = jnp.mean(x, axis=-1, keepdims=True)
        var = jnp.var(x, axis=-1, keepdims=True)
        xn = (x - mean) / jnp.sqrt(var + 1e-05)
        out = xn.reshape(bs * seq, DIM) * gn_w + gn_b
        return out.reshape(bs, seq, DIM)

    def _L0_ffn_ref(x, ln_gamma, ln_beta, mu, scale, w1, b1, w2, b2):
        import jax, jax.numpy as jnp
        import numpy as np
        LN_EPS = 1e-05
        NORM_EPS = 1e-12

        def _layernorm(x, gamma, beta):
            mu = x.mean(axis=-1, keepdims=True)
            var = ((x - mu) ** 2).mean(axis=-1, keepdims=True)
            return (x - mu) * jax.lax.rsqrt(var + LN_EPS) * gamma + beta

        def _l2norm(x, axis):
            n = jnp.sqrt((x ** 2).sum(axis=axis, keepdims=True))
            return x / jnp.maximum(n, NORM_EPS)
        B, N, D = x.shape
        _, E, S = mu.shape
        xn = _layernorm(x, ln_gamma, ln_beta)
        x_unit = _l2norm(xn, axis=-1)
        mu_unit = _l2norm(mu, axis=0)
        logits = jnp.einsum('bnd,des->bnes', x_unit * scale, mu_unit)
        dispatch = jax.nn.softmax(logits, axis=1)
        combine = jax.nn.softmax(logits.reshape(B, N, E * S), axis=-1).reshape(B, N, E, S)
        slot_in = jnp.einsum('bnd,bnes->besd', xn, dispatch)
        h = jax.nn.gelu(jnp.einsum('besd,edh->besh', slot_in, w1) + b1[None, :, None, :], approximate=False)
        slot_out = jnp.einsum('besh,ehd->besd', h, w2) + b2[None, :, None, :]
        out = jnp.einsum('besd,bnes->bnd', slot_out, combine)
        return out
    x = x + _L0_xattn_ref(_layernorm(x, axis=-1), ctx_1024, ctx_1024, L0_xattn_Wi_w, L0_xattn_Wi_b, L0_xattn_Wf_w, L0_xattn_Wf_b, L0_xattn_gn_w, L0_xattn_gn_b)
    x = x + _L0_ffn_ref(_layernorm(x, axis=-1), L0_ffn_ln_gamma, L0_ffn_ln_beta, L0_ffn_mu, L0_ffn_scale, L0_ffn_w1, L0_ffn_b1, L0_ffn_w2, L0_ffn_b2)
    return x

_drawn_inputs = setup_inputs


def setup_inputs(seed=0):
    import zlib

    import numpy as np

    out = dict(_drawn_inputs(seed))
    spreads = {'L0_xattn_Wi_w': (0.0, 0.1),
     'L0_xattn_Wf_w': (0.0, 0.1),
     'L0_xattn_gn_w': (1.0, 0.2),
     'L0_xattn_gn_b': (0.0, 0.1),
     'L0_ffn_ln_gamma': (1.0, 0.6),
     'L0_ffn_ln_beta': (0.0, 0.8),
     'L0_ffn_b1': (0.0, 0.8),
     'L0_ffn_b2': (0.0, 0.515)}
    factors = {'L0_xattn_Wi_b': 64.0, 'L0_ffn_mu': 31.235, 'L0_ffn_w1': 6.047, 'L0_ffn_w2': 5.469}
    for name, (base, spread) in spreads.items():
        noise = np.random.default_rng([zlib.crc32(name.encode()), seed]).standard_normal(out[name].shape)
        drawn = base * np.exp(spread * noise) if base else spread * noise
        out[name] = jnp.asarray(drawn.astype(out[name].dtype))
    for name, factor in factors.items():
        out[name] = (out[name] * factor).astype(out[name].dtype)
    return out
```

```python
from contextlib import ExitStack

import numpy as np

import concourse.bass as bass
from concourse import mybir

F32 = mybir.dt.float32
F32R = mybir.dt.float32r
ALU = mybir.AluOpType
ACT = mybir.ActivationFunctionType
AX = mybir.AxisListType

P = 128
TAU = 32.0 ** 0.5
LN_EPS = 1e-5
NORM_FLOOR_SQ = 1e-24
NEG_BIG = -3.0e38


def xattn_ffn(nc, x, ctx_in, Wi_w, Wi_b, Wf_w, Wf_b, gn_w, gn_b,
              ln_gamma, ln_beta, mu, scale, w1, b1, w2, b2, out):
    NB, SEQ, D = x.shape
    H = Wi_w.shape[0]
    HD = D // H
    V1 = HD + 1
    NC = SEQ // P
    NT = NB * NC
    _, E, S = mu.shape
    HID = w1.shape[2]
    ES = E * S
    DC = D // P
    EC = ES // P
    EP = E // 2
    BH = NB * H
    HPC = P // HD
    EPC = P // S
    assert NC == 2 and DC == 2 and EC == 2 and H == 8 and HID == 64 and NB * S == P

    with ExitStack() as stack:
        def sb(name, shape, dt=F32):
            return stack.enter_context(nc.sbuf_tensor(name, shape, dt))

        def sem(name):
            return stack.enter_context(nc.semaphore(name))

        X = sb("X", [P, NT, D])
        CX = sb("CX", [P, NT * D])
        ctx_t = CX[:].rearrange("p (t d) -> p t d", t=NT)
        DEC = CX[:].rearrange("p (u c h i) -> p u c h i", u=2, c=NC, h=H)
        SIN = CX[:].rearrange("p (k e b s) -> p k e b s", k=DC, e=E, b=NB)
        VE = sb("VE", [P, NT, H, V1])
        ECT = VE[:].rearrange("p t h v -> p (t h v)")[:, 0:NB * EC * SEQ].rearrange(
            "p (b k n) -> p b k n", b=NB, k=EC)
        Q = sb("Q", [P, NT, D])
        QKT = sb("QKT", [P, NT, 2 * DC, P])
        flat = QKT[:].rearrange("p t k n -> p (t k n)")
        W = NC * D
        XN = flat[:, 0:4 * W].rearrange("p (u c d) -> p u c d", u=4, c=NC)
        XNT = flat[:, 4 * W:6 * W].rearrange("p (u k n) -> p u k n", u=2, k=DC)
        LSB = flat[:, 6 * W:8 * W].rearrange("p (u c e) -> p u c e", u=2, c=NC)
        ECB = flat[:, 8 * W:10 * W].rearrange("p (u c e) -> p u c e", u=2, c=NC)
        EDT = flat[:, 10 * W:12 * W].rearrange("p (u k n) -> p u k n", u=2, k=EC)
        ED = flat[:, 12 * W:14 * W].rearrange("p (u c e) -> p u c e", u=2, c=NC)
        SOT = flat[:, 0:DC * E * P].rearrange("p (k b e s) -> p k b e s", k=DC, b=NB, e=E)
        o = DC * E * P
        HS = flat[:, o:o + EP * P].rearrange("p (e n) -> p e n", e=EP)
        SO = flat[:, o + 2 * W:o + 4 * W].rearrange("p (u k d) -> p u k d", u=2, k=EC)
        Y = flat[:, o + 4 * W:o + 6 * W].rearrange("p (u c d) -> p u c d", u=2, c=NC)
        MROW = sb("MROW", [4, 2, H, SEQ], F32R)
        GROW = sb("GROW", [4, 2, H, SEQ], F32R)
        MHL = sb("MHL", [BH, 2, SEQ], F32R)
        GHL = sb("GHL", [BH, 2, SEQ], F32R)
        ident = sb("ident", [P, P])
        ones = sb("ones", [P, P])
        blockmask = sb("blockmask", [P, HPC * V1])
        eps = sb("eps", [P, 1])
        neghalf = sb("neghalf", [P, NC * H])
        GNW = sb("GNW", [P, D])
        GNB = sb("GNB", [P, D])
        GAM = sb("GAM", [P, D])
        BET = sb("BET", [P, D])
        SCL = sb("SCL", [P, 1])
        BG = sb("BG", [P, 2, H])
        WW = sb("WW", [2 * H, 3 * D])
        WTA = sb("WTA", [P, 6, 2 * H])
        WT = sb("WT", [P, 4, 2 * H])
        B1L = sb("B1L", [EP, P])
        B1 = sb("B1", [P, EP])
        B2R = sb("B2R", [P, EC, D])
        W1 = sb("W1", [P, DC, E, HID])
        W2 = sb("W2", [P, EP, D])
        MU = sb("MU", [P, DC, ES])
        MUQ = sb("MUQ", [P, DC, ES])
        MUN = sb("MUN", [P, ES])
        ST = sb("ST", [P, NT, 6])
        MV = sb("MV", [P, NT, 2])
        LV = sb("LV", [P, NT])
        RS = sb("RS", [P, NT])
        G1 = sb("G1", [P, 2, NC, BH])
        FS = sb("FS", [BH, SEQ])
        NA = sb("NA", [BH, SEQ])
        EF = sb("EF", [BH, SEQ])
        LF = sb("LF", [BH, SEQ])
        LS = sb("LS", [BH, SEQ])
        CS = sb("CS", [BH, SEQ])
        G = sb("G", [BH, SEQ])
        M = sb("M", [BH, SEQ])
        NM = sb("NM", [BH, SEQ])
        CM = sb("CM", [BH, SEQ])
        ROWS = sb("ROWS", [BH, 4, P])
        TT = sb("TT", [P, 4, BH])
        EK = sb("EK", [P, 2, H, HD])
        KVS = sb("KVS", [P, 2, HPC * V1])
        HT1 = sb("HT1", [P, H, V1])
        HB = sb("HB", [P, 2, NC, H, V1])
        HC = sb("HC", [P, 2, NC, H, HD])
        SQ = sb("SQ", [P, NC, H, HD])
        SM = sb("SM", [P, 2, 10, NC * H])
        NRM = sb("NRM", [P, 2, NC, D])
        XH = sb("XH", [P, 2, NC, D])
        JNK = sb("JNK", [P, D])
        SS = sb("SS", [P, NB, 8, NC])
        RC = sb("RC", [P, NB, NC])
        RCI = sb("RCI", [P, NB, NC])
        DM = sb("DM", [P, NB, EC])
        DS = sb("DS", [P, NB, EC])
        DR = sb("DR", [P, NB, EC])
        PS = stack.enter_context(nc.psum_tensor("PS", [P, 8, 512], F32))

        x_in = [sem(f"x_in{b}") for b in range(NB)]
        c_in = [sem(f"c_in{b}") for b in range(NB)]
        w_in = sem("w_in")
        mu_in = sem("mu_in")
        vec_in = sem("vec_in")
        moe_in = sem("moe_in")

        rows_in = [sem("rows_in0"), sem("rows_in1")]
        y_out = [sem("y_out0"), sem("y_out1")]
        consts = sem("consts")
        const_step = sem("const_step")
        wT_ps = sem("wT_ps")
        wt_step = sem("wt_step")
        b1_sb = sem("b1_sb")
        musq = sem("musq")
        mu_sum = sem("mu_sum")
        mu_max = sem("mu_max")
        mu_sqrt = sem("mu_sqrt")
        mu_step = sem("mu_step")
        ln_st = sem("ln_st")
        ln_mv = sem("ln_mv")
        ln_var = sem("ln_var")
        ln_rs = sem("ln_rs")
        q_sb = sem("q_sb")
        qk_ps = sem("qk_ps")
        qk_sb = sem("qk_sb")
        ve_ones = sem("ve_ones")
        ve_sb = sem("ve_sb")
        gate_ps = sem("gate_ps")
        gate_sb = sem("gate_sb")
        gateT_ps = sem("gateT_ps")
        row_step = sem("row_step")
        sig_e = sem("sig_e")
        sig_l = sem("sig_l")
        tok_rows = sem("tok_rows")
        split = sem("split")
        rowsT_ps = sem("rowsT_ps")
        rowsT_sb = sem("rowsT_sb")
        arg_ps = sem("arg_ps")
        dec_sb = sem("dec_sb")
        dec_mask = sem("dec_mask")
        s_ps = sem("s_ps")
        c_sb = sem("c_sb")
        ek_sb = sem("ek_sb")
        kv_ps = sem("kv_ps")
        kv_sb = sem("kv_sb")
        ho_ps = sem("ho_ps")
        ho_sb = sem("ho_sb")
        hd_ps = sem("hd_ps")
        h0_sb = sem("h0_sb")
        h1_sb = sem("h1_sb")
        post_step = sem("post_step")
        sq_sb = sem("sq_sb")
        gn_var = sem("gn_var")
        gn_rs = sem("gn_rs")
        nrm_sb = sem("nrm_sb")
        xb_sb = sem("xb_sb")
        gw_sb = sem("gw_sb")
        x1_sb = sem("x1_sb")
        l_st = sem("l_st")
        l_mv = sem("l_mv")
        l_var = sem("l_var")
        l_rs = sem("l_rs")
        xh_sb = sem("xh_sb")
        xg_sb = sem("xg_sb")
        xn_sb = sem("xn_sb")
        ss_sb = sem("ss_sb")
        rn_step = sem("rn_step")
        rn_sb = sem("rn_sb")
        xnT_ps = sem("xnT_ps")
        xnT_sb = sem("xnT_sb")
        l_ps = sem("l_ps")
        l_sb = sem("l_sb")
        rowmax_sb = sem("rowmax_sb")
        ec_sb = sem("ec_sb")
        lT_ps = sem("lT_ps")
        colmax_sb = sem("colmax_sb")
        edt_sb = sem("edt_sb")
        edt_step = sem("edt_step")
        edt_n = sem("edt_n")
        edT_ps = sem("edT_ps")
        ed_sb = sem("ed_sb")
        ecT_ps = sem("ecT_ps")
        ecT_sb = sem("ecT_sb")
        rc_sb = sem("rc_sb")
        slot_ps = sem("slot_ps")
        slot_sb = sem("slot_sb")
        hid_ps = sem("hid_ps")
        hid_sb = sem("hid_sb")
        so_ps = sem("so_ps")
        soa_sb = sem("soa_sb")
        sov_sb = sem("sov_sb")
        soT_ps = sem("soT_ps")
        so_sb = sem("so_sb")
        y_ps = sem("y_ps")
        y_sb = sem("y_sb")

        block = stack.enter_context(nc.Block())

        @block.sync
        def _(sp):
            def bc(v, n=P):
                return v.partition_broadcast(n)

            def tok(a, b):
                return a[b].rearrange("(c p) d -> p c d", p=P)
            sp.dma_start(X[:, 0:NC, :], tok(x, 0)).then_inc(x_in[0], 16)
            sp.dma_start(ctx_t[:, 0:NC, :], tok(ctx_in, 0)).then_inc(c_in[0], 16)
            sp.dma_start(WW[0:H, :], Wi_w).then_inc(w_in, 16)
            sp.dma_start(WW[H:2 * H, :], Wf_w).then_inc(w_in, 16)
            sp.dma_start(B1L[:], b1.rearrange("(p q) h -> p (q h)", q=2)).then_inc(w_in, 16)
            for b in range(1, NB):
                sp.dma_start(X[:, NC * b:NC * b + NC, :], tok(x, b)).then_inc(x_in[b], 16)
                sp.dma_start(ctx_t[:, NC * b:NC * b + NC, :], tok(ctx_in, b)).then_inc(c_in[b], 16)
            sp.dma_start(MU[:], mu.rearrange("(k p) e s -> p k (e s)", p=P)).then_inc(mu_in, 16)
            sp.dma_start(BG[:, 0, :], bc(Wi_b)).then_inc(vec_in, 16)
            sp.dma_start(BG[:, 1, :], bc(Wf_b)).then_inc(vec_in, 16)
            sp.dma_start(GNW[:], bc(gn_w)).then_inc(vec_in, 16)
            sp.dma_start(GNB[:], bc(gn_b)).then_inc(vec_in, 16)
            sp.dma_start(GAM[:], bc(ln_gamma)).then_inc(vec_in, 16)
            sp.dma_start(BET[:], bc(ln_beta)).then_inc(vec_in, 16)
            sp.dma_start(SCL[:], bc(scale)).then_inc(vec_in, 16)
            for k in range(DC):
                sp.dma_start(W1[:, k], w1[:, k * P:(k + 1) * P, :].rearrange("e p h -> p e h")).then_inc(moe_in, 16)
            for q in range(2):
                sp.dma_start(W2[q * HID:(q + 1) * HID], w2.rearrange("(p q) h d -> q h p d", q=2)[q]).then_inc(moe_in, 16)
            for k in range(EC):
                for e in range(EPC):
                    sp.dma_start(B2R[e * S:(e + 1) * S, k, :], bc(b2[k * EPC + e], S)).then_inc(moe_in, 16)
            sp.wait_ge(split, 4)
            sp.wait_ge(consts, 7)
            for b in range(NB):
                if b >= 2:
                    sp.wait_ge(arg_ps, 4 * (b - 1))
                for a in range(2):
                    sp.dma_start(MROW[a:a + 1, b % 2].bitcast(F32), MHL[H * b:H * b + H, a, :].bitcast(F32)).then_inc(rows_in[b % 2], 16)
                    sp.dma_start(GROW[2 + a:3 + a, b % 2].bitcast(F32), GHL[H * b:H * b + H, a, :].bitcast(F32)).then_inc(rows_in[b % 2], 16)
            for b in range(NB):
                sp.wait_ge(y_sb, NC * (b + 1))
                sp.dma_start(out[b].rearrange("(c p) d -> p c d", p=P), Y[:, b % 2]).then_inc(y_out[b % 2], 16)
            sp.wait_ge(y_out[0], 16 * (NB // 2))
            sp.wait_ge(y_out[1], 16 * (NB // 2))

        @block.gpsimd
        def _(pool):
            pool.memset(ident[:], 1.0).then_inc(const_step, 1)
            pool.memset(ones[:], 1.0).then_inc(consts, 1)
            pool.memset(MROW[:].bitcast(F32), 1.0).then_inc(consts, 1)
            pool.memset(GROW[:].bitcast(F32), 1.0).then_inc(consts, 1)
            pool.memset(eps[:], LN_EPS).then_inc(consts, 1)
            pool.memset(neghalf[:], -0.5).then_inc(consts, 1)
            pool.memset(blockmask[:], 1.0).then_inc(const_step, 1)
            pool.wait_ge(const_step, 2)
            pool.affine_select(out=ident[:], in_=ident[:], compare_op=ALU.is_equal, fill=0.0, base=0,
                               pattern=[[-1, P]], channel_multiplier=1).then_inc(consts, 1)
            bm = blockmask[:].rearrange("p (r v) -> p r v", r=HPC)
            pool.affine_select(out=bm, in_=bm, compare_op=ALU.is_ge, fill=0.0, base=0,
                               pattern=[[-HD, HPC], [0, V1]], channel_multiplier=1).then_inc(const_step, 1)
            pool.wait_ge(const_step, 3)
            pool.affine_select(out=bm, in_=bm, compare_op=ALU.is_gt, fill=0.0, base=HD,
                               pattern=[[HD, HPC], [0, V1]], channel_multiplier=-1).then_inc(consts, 1)
            pool.wait_ge(consts, 7)
            pool.memset(VE[:, :, :, HD:V1], 1.0).then_inc(ve_ones, 1)
            for b in range(NB):
                t = NC * b
                pool.wait_ge(ln_mv, t + NC)
                pool.tensor_scalar(LV[:, t:t + NC], MV[:, t:t + NC, 1], 1.0, LN_EPS, ALU.mult, ALU.add).then_inc(ln_var, 1)
                pool.wait_ge(ln_var, b + 1)
                pool.tensor_tensor(RS[:, t:t + NC], LV[:, t:t + NC], neghalf[:, 0:NC], ALU.pow).then_inc(ln_rs, 1)
                pool.wait_ge(c_in[b], 16)
                for t in (NC * b, NC * b + 1):
                    pool.tensor_scalar(VE[:, t, :, 0:HD], ctx_t[:, t].rearrange("p (h v) -> p h v", h=H),
                                       1.0, 0.0, ALU.mult, ALU.add).then_inc(ve_sb, 1)
            pool.wait_ge(mu_in, 16)
            pool.tensor_tensor(MUQ[:], MU[:], MU[:], ALU.mult).then_inc(musq, 1)

            def ev(b):
                if b == 0:
                    pool.wait_ge(rowsT_sb, 1)
                    pool.wait_ge(ve_sb, NT)
                    pool.wait_ge(ve_ones, 1)
                if b >= 2:
                    pool.wait_ge(kv_ps, b - 1)
                e = TT[:, 2, H * b:H * b + H].unsqueeze(2).to_broadcast([P, H, HD])
                pool.tensor_tensor(EK[:, b % 2], VE[:, NC * b, :, 0:HD], e, ALU.mult).then_inc(ek_sb, 1)

            def masks(b):
                for c in range(NC):
                    pool.wait_ge(dec_sb, 4 * b + 2 * c + 2)
                    d = DEC[:, b % 2, c]
                    pool.affine_select(out=d, in_=d, compare_op=ALU.is_ge, fill=0.0, base=0,
                                       pattern=[[0, H], [1, P]], channel_multiplier=-1).then_inc(dec_mask, 1)

            def head_rs(b):
                u = b % 2
                pool.wait_ge(post_step, 12 * b + 10)
                pool.tensor_scalar(SM[:, u, 7], SM[:, u, 6], 1.0, LN_EPS, ALU.mult, ALU.add).then_inc(gn_var, 1)
                pool.wait_ge(gn_var, b + 1)
                pool.tensor_tensor(SM[:, u, 8], SM[:, u, 7], neghalf[:], ALU.pow).then_inc(gn_rs, 1)

            def residual(b):
                u = b % 2
                if b == 0:
                    pool.wait_ge(vec_in, 16 * 7)
                xb = X[:, NC * b:NC * b + NC, :]
                pool.wait_ge(q_sb, NT)
                pool.tensor_tensor(xb, xb, GNB[:].unsqueeze(1).to_broadcast([P, NC, D]), ALU.add).then_inc(xb_sb, 1)
                pool.wait_ge(nrm_sb, b + 1)
                pool.tensor_tensor(NRM[:, u], NRM[:, u], GNW[:].unsqueeze(1).to_broadcast([P, NC, D]),
                                   ALU.mult).then_inc(gw_sb, 1)
                pool.wait_ge(gw_sb, b + 1)
                pool.wait_ge(xb_sb, b + 1)
                pool.wait_ge(qk_ps, NT)
                pool.tensor_tensor(Q[:, NC * b:NC * b + NC, :], NRM[:, u], xb, ALU.add).then_inc(x1_sb, 1)

            ev(0)
            for b in range(NB + 1):
                if b < NB:
                    masks(b)
                    if b + 1 < NB:
                        ev(b + 1)
                if b >= 1:
                    head_rs(b - 1)
                    residual(b - 1)

            def affine(b):
                u = b % 2
                pool.wait_ge(xh_sb, NC * (b + 1))
                if b >= 4:
                    pool.wait_ge(slot_ps, b - 3)
                if b == 0:
                    pool.wait_ge(hd_ps, 2 * NB)
                    pool.wait_ge(ho_ps, NB)
                pool.tensor_tensor(XN[:, b % 4], XH[:, u], GAM[:].unsqueeze(1).to_broadcast([P, NC, D]),
                                   ALU.mult).then_inc(xg_sb, 1)
                pool.wait_ge(xg_sb, b + 1)
                pool.tensor_tensor(XN[:, b % 4], XN[:, b % 4], BET[:].unsqueeze(1).to_broadcast([P, NC, D]),
                                   ALU.add).then_inc(xn_sb, 1)

            def norm(b):
                pool.wait_ge(ss_sb, NC * (b + 1))
                pool.tensor_scalar(SS[:, b, 1], SS[:, b, 0], NORM_FLOOR_SQ, 0.0, ALU.max, ALU.add).then_inc(rn_step, 1)
                pool.wait_ge(rn_step, 2 * b + 1)
                pool.tensor_tensor(SS[:, b, 2], SS[:, b, 1], neghalf[:, 0:NC], ALU.pow).then_inc(rn_step, 1)
                pool.wait_ge(rn_step, 2 * b + 2)
                pool.tensor_tensor(SS[:, b, 3], SS[:, b, 2], SCL[:].to_broadcast([P, NC]), ALU.mult).then_inc(rn_sb, 1)

            def lnrs(b):
                pool.wait_ge(l_var, b + 1)
                pool.tensor_tensor(SS[:, b, 6], SS[:, b, 4], neghalf[:, 0:NC], ALU.pow).then_inc(l_rs, 1)

            lnrs(0)
            for k in range(NB + 1):
                if k + 1 < NB:
                    lnrs(k + 1)
                if k < NB:
                    affine(k)
                if k >= 1:
                    norm(k - 1)

        @block.scalar
        def _(act):
            act.wait_ge(consts, 7)
            for b in range(1, NB + 1):
                for t in (NC * b - 2, NC * b - 1):
                        act.wait_ge(qk_ps, t + 1)
                        act.copy(QKT[:, t].rearrange("p k n -> p (k n)"), PS[:, t % 2, :]).then_inc(qk_sb, 1)
            act.wait_ge(row_step, 2)
            act.activation(EF[:], NA[:], ACT.Exp).then_inc(sig_e, 1)
            act.wait_ge(sig_e, 1)
            act.activation(LF[:], EF[:], ACT.Ln, bias=ones[0:BH, 0:1]).then_inc(sig_l, 1)
            act.wait_ge(row_step, 8)
            act.activation(ROWS[:, 2, :], G[:, 0:P], ACT.Exp, bias=NM[:, P - 1:P]).then_inc(tok_rows, 1)
            act.activation(ROWS[:, 3, :], NM[:, P:SEQ], ACT.Exp, bias=M[:, P - 1:P]).then_inc(tok_rows, 1)
            act.activation(ROWS[:, 0:2, :], CM[:].rearrange("r (c i) -> r c i", c=NC), ACT.Exp,
                           scale=-1.0).then_inc(tok_rows, 1)
            act.wait_ge(mu_max, 1)
            act.activation(MUN[:], MUN[:], ACT.Sqrt).then_inc(mu_sqrt, 1)

            def decay(b):
                for k in range(4 * b, 4 * b + 4):
                    c, half = (k // 2) % 2, k % 2
                    act.wait_ge(arg_ps, k + 1)
                    if b == 0 and k == 0:
                        act.wait_ge(ve_sb, NT)
                        act.wait_ge(qk_ps, NT)
                    if b >= 2:
                        act.wait_ge(hd_ps, 2 * (b - 2) + 2)
                    act.activation(DEC[:, b % 2, c, 4 * half:4 * half + 4, :],
                                   PS[:, 4 + k % 2, :].rearrange("p (h i) -> p h i", h=4),
                                   ACT.Exp).then_inc(dec_sb, 1)

            def h0(b):
                act.wait_ge(hd_ps, 2 * b + 1)
                if b >= 2:
                    act.wait_ge(post_step, 12 * (b - 1))
                act.copy(HB[:, b % 2, 0], PS[:, 6, 0:H * V1].rearrange("p (h v) -> p h v", h=H)).then_inc(h0_sb, 1)

            def post_a(b):
                u = b % 2
                act.wait_ge(post_step, 12 * b + 7)
                if b >= 1:
                    act.wait_ge(post_step, 12 * b - 2)
                act.activation(SQ[:], HC[:, u], ACT.Square).then_inc(sq_sb, 1)

            decay(0)
            for b in range(NB):
                h0(b)
                if b + 1 < NB:
                    decay(b + 1)
                post_a(b)

            def sqn(b):
                act.wait_ge(xn_sb, b + 1)
                for c in range(NC):
                    if b or c:
                        act.wait_ge(ss_sb, NC * b + c)
                    act.activation(JNK[:], XN[:, b % 4, c], ACT.Square, accum_out=SS[:, b, 0, c:c + 1]).then_inc(ss_sb, 1)

            def xnt(b):
                act.wait_ge(xnT_ps, b + 1)
                if b >= 2:
                    act.wait_ge(l_ps, b - 1)
                act.copy(XNT[:, b % 2].rearrange("p k n -> p (k n)"), PS[:, 0, :]).then_inc(xnT_sb, 1)

            def lsb(b):
                act.wait_ge(l_ps, b + 1)
                act.wait_ge(rn_sb, b + 1)
                if b >= 2:
                    act.wait_ge(lT_ps, b - 1)
                for c in range(NC):
                    act.activation(LSB[:, b % 2, c], PS[:, 1, c * ES:(c + 1) * ES], ACT.Copy,
                                   scale=SS[:, b, 3, c:c + 1]).then_inc(l_sb, 1)

            def ecb(b):
                act.wait_ge(rowmax_sb, b + 1)
                if b >= 2:
                    act.wait_ge(ecT_ps, b - 1)
                for c in range(NC):
                    act.activation(ECB[:, b % 2, c], LSB[:, b % 2, c], ACT.Exp, bias=SS[:, b, 7, c:c + 1],
                                   accum_out=RC[:, b, c:c + 1]).then_inc(ec_sb, 1)

            def edt(b):
                act.wait_ge(colmax_sb, b + 1)
                if b >= 2:
                    act.wait_ge(edT_ps, b - 1)
                for k in range(EC):
                    act.activation(EDT[:, b % 2, k], PS[:, 2, k * SEQ:(k + 1) * SEQ], ACT.Exp,
                                   bias=DM[:, b, k:k + 1], accum_out=DS[:, b, k:k + 1]).then_inc(edt_sb, 1)

            def slot(b):
                act.wait_ge(slot_ps, b + 1)
                if b == 0:
                    act.wait_ge(hd_ps, 2 * NB)
                act.copy(SIN[:, :, :, b, :], PS[:, 5, :].rearrange("p (k e s) -> p k e s", k=DC, e=E)).then_inc(slot_sb, 1)

            for k in range(NB + 4):
                if k < NB:
                    sqn(k)
                    xnt(k)
                if 1 <= k <= NB:
                    lsb(k - 1)
                    ecb(k - 1)
                if 2 <= k <= NB + 1:
                    edt(k - 2)
                if 4 <= k:
                    slot(k - 4)
            for p in range(EP):
                act.wait_ge(hid_ps, 4 * (p // 4 + 1))
                if p == 0:
                    act.wait_ge(b1_sb, 1)
                act.activation(HS[:, p], PS[:, p // 4, (p % 4) * P:(p % 4 + 1) * P], ACT.Gelu,
                               bias=B1[:, p:p + 1]).then_inc(hid_sb, 1)
            for k in range(DC):
                for pp in range(2):
                    act.wait_ge(so_ps, k + 1)
                    bank = (2 + 4 * k + 2 * 0 + pp) % 8
                    act.copy(SOT[:, k, :, 8 * pp:8 * pp + 8:2, :].rearrange("p b e s -> p e b s"),
                             PS[:, bank, :].rearrange("p (e b s) -> p e b s", e=4, b=NB)).then_inc(soa_sb, 1)

        @block.tensor
        def _(pe):
            pe.wait_ge(consts, 7)
            pe.wait_ge(w_in, 48)
            for k in range(6):
                pe.transpose(PS[:, 3, k * 16:(k + 1) * 16], WW[:, k * P:(k + 1) * P],
                             ident[0:16, 0:16]).then_inc(wT_ps, 1)
            pe.transpose(PS[:, 3, 96:96 + EP], B1L[:], ident[0:EP, 0:EP]).then_inc(wT_ps, 1)

            def gates(t):
                pe.wait_ge(qk_sb, t + 1)
                for k in range(4):
                    mm = pe.matmul(PS[:, 2, t * 16:(t + 1) * 16], QKT[:, t, k], WT[:, k], start=(k == 0), stop=(k == 3))
                mm.then_inc(gate_ps, 1)

            for t in range(NT):
                pe.wait_ge(q_sb, t + 1)
                pe.wait_ge(c_in[t // NC], 16)
                if t >= 2:
                    pe.wait_ge(qk_sb, t - 1)
                for k in range(DC):
                    pe.transpose(PS[:, t % 2, k * P:(k + 1) * P], Q[:, t, k * P:(k + 1) * P], ident[:])
                for k in range(DC):
                    tr = pe.transpose(PS[:, t % 2, (DC + k) * P:(DC + k + 1) * P], ctx_t[:, t, k * P:(k + 1) * P], ident[:])
                tr.then_inc(qk_ps, 1)
                if t == 2:
                    pe.wait_ge(wt_step, 3)
                if t >= 2:
                    gates(t - 2)
            gates(NT - 2)
            gates(NT - 1)
            pe.wait_ge(musq, 1)
            pe.wait_ge(b1_sb, 1)
            for k in range(DC):
                mm = pe.matmul(PS[:, 3, 0:ES], ones[:], MUQ[:, k], start=(k == 0), stop=(k == DC - 1))
            mm.then_inc(mu_sum, 1)
            pe.wait_ge(gate_sb, 2)
            for g in range(2):
                for c in range(NC):
                    tr = pe.transpose(PS[0:BH, 4, (2 * g + c) * P:(2 * g + c + 1) * P], G1[:, g, c, :], ident[:])
            tr.then_inc(gateT_ps, 1)
            pe.wait_ge(tok_rows, 3)
            for r in range(4):
                tr = pe.transpose(PS[:, 5, r * BH:(r + 1) * BH], ROWS[:, r, :], ident[0:BH, 0:BH])
            tr.then_inc(rowsT_ps, 1)

            def args(b, lo, hi):
                if lo == 0:
                    pe.wait_ge(rows_in[b % 2], 64 * (b // 2 + 1))
                    if b == 0:
                        pe.wait_ge(row_step, 8)
                        pe.wait_ge(rowsT_sb, 1)
                for k in range(4 * b + lo, 4 * b + hi):
                    c, half = (k // 2) % 2, k % 2
                    if k >= 2:
                        pe.wait_ge(dec_sb, k - 1)
                    for j in range(4):
                        h = 4 * half + j
                        mm = pe.matmul(PS[:, 4 + k % 2, j * P:(j + 1) * P], GROW[0:4, b % 2, h, c * P:(c + 1) * P],
                                       MROW[0:4, b % 2, h, c * P:(c + 1) * P], start=True, stop=True)
                    mm.then_inc(arg_ps, 1)

            def scores(b):
                if b == 0:
                    pe.wait_ge(qk_sb, NT)
                    pe.wait_ge(gate_sb, 2)
                    pe.wait_ge(mu_max, 1)
                if b >= 1:
                    pe.wait_ge(c_sb, NC * b)
                for c in range(NC):
                    for hh in range(H // HPC):
                        for r in range(HPC):
                            rows = slice(HD * r, HD * r + HD)
                            mm = pe.matmul(PS[:, r, (2 * c + hh) * P:(2 * c + hh + 1) * P],
                                           QKT[rows, NC * b + c, DC + hh, :], QKT[rows, NC * b + c, hh, :],
                                           start=True, stop=True)
                mm.then_inc(s_ps, 1)

            def state(b):
                pe.wait_ge(ek_sb, b + 1)
                if b >= 1:
                    pe.wait_ge(ho_sb, b)
                for hh in range(H // HPC):
                    mm = pe.matmul(PS[:, 7, hh * HPC * V1:(hh + 1) * HPC * V1],
                                   EK[:, b % 2, hh * HPC:(hh + 1) * HPC, :],
                                   VE[:, NC * b, hh * HPC:(hh + 1) * HPC, :].rearrange("p h v -> p (h v)"),
                                   start=True, stop=True)
                mm.then_inc(kv_ps, 1)

            def apply(b):
                pe.wait_ge(kv_sb, b + 1)
                for hh in range(H // HPC):
                    mm = pe.matmul(PS[:, 7, hh * HPC * V1:(hh + 1) * HPC * V1], QKT[:, NC * b + 1, hh, :],
                                   KVS[:, hh, :], start=True, stop=True)
                mm.then_inc(ho_ps, 1)

            def pv(b, c):
                pe.wait_ge(c_sb, NC * b + c + 1)
                if c == 1:
                    pe.wait_ge(h0_sb, b + 1)
                elif b >= 1:
                    pe.wait_ge(h1_sb, b)
                for h in range(H):
                    mm = pe.matmul(PS[:, 6, h * V1:(h + 1) * V1], DEC[:, b % 2, c, h, :], VE[:, NC * b + c, h, :],
                                   start=True, stop=True)
                mm.then_inc(hd_ps, 1)

            args(0, 0, 4)
            scores(0)
            state(0)
            for b in range(NB):
                if b + 1 < NB:
                    args(b + 1, 0, 2)
                pv(b, 0)
                apply(b)
                if b + 1 < NB:
                    args(b + 1, 2, 4)
                pv(b, 1)
                if b + 1 < NB:
                    scores(b + 1)
                    state(b + 1)

            def p_xnT(b):
                pe.wait_ge(xn_sb, b + 1)
                if b >= 1:
                    pe.wait_ge(xnT_sb, b)
                if b == 0:
                    pe.wait_ge(c_sb, NT)
                    pe.wait_ge(dec_sb, 4 * NB)
                    pe.wait_ge(mu_step, 2)
                for k in range(DC):
                    for c in range(NC):
                        tr = pe.transpose(PS[:, 0, k * SEQ + c * P:k * SEQ + (c + 1) * P],
                                          XN[:, b % 4, c, k * P:(k + 1) * P], ident[:])
                tr.then_inc(xnT_ps, 1)

            def p_l(b):
                pe.wait_ge(xnT_sb, b + 1)
                if b >= 1:
                    pe.wait_ge(l_sb, NC * b)
                for c in range(NC):
                    for k in range(DC):
                        mm = pe.matmul(PS[:, 1, c * ES:(c + 1) * ES], XNT[:, b % 2, k, c * P:(c + 1) * P], MU[:, k],
                                       start=(k == 0), stop=(k == DC - 1))
                mm.then_inc(l_ps, 1)

            def p_lT(b):
                pe.wait_ge(l_sb, NC * (b + 1))
                if b >= 1:
                    pe.wait_ge(edt_sb, EC * b)
                for k in range(EC):
                    for c in range(NC):
                        tr = pe.transpose(PS[:, 2, k * SEQ + c * P:k * SEQ + (c + 1) * P],
                                          LSB[:, b % 2, c, k * P:(k + 1) * P], ident[:])
                tr.then_inc(lT_ps, 1)

            def p_ecT(b):
                pe.wait_ge(ec_sb, NC * (b + 1))
                if b >= 1:
                    pe.wait_ge(ecT_sb, b)
                for k in range(EC):
                    for c in range(NC):
                        tr = pe.transpose(PS[:, 4, k * SEQ + c * P:k * SEQ + (c + 1) * P],
                                          ECB[:, b % 2, c, k * P:(k + 1) * P], ident[:])
                tr.then_inc(ecT_ps, 1)

            def p_edT(b):
                pe.wait_ge(edt_n, EC * (b + 1))
                if b >= 1:
                    pe.wait_ge(ed_sb, b)
                for c in range(NC):
                    for k in range(EC):
                        tr = pe.transpose(PS[:, 3, c * ES + k * P:c * ES + (k + 1) * P],
                                          EDT[:, b % 2, k, c * P:(c + 1) * P], ident[:])
                tr.then_inc(edT_ps, 1)

            def p_slot(b):
                pe.wait_ge(ed_sb, b + 1)
                if b >= 1:
                    pe.wait_ge(slot_sb, b)
                for k in range(DC):
                    for c in range(NC):
                        mm = pe.matmul(PS[:, 5, k * ES:(k + 1) * ES], XN[:, b % 4, c, k * P:(k + 1) * P], ED[:, b % 2, c],
                                       start=(c == 0), stop=(c == NC - 1))
                mm.then_inc(slot_ps, 1)

            for k in range(NB + 4):
                if k < NB:
                    p_xnT(k)
                if 1 <= k <= NB:
                    p_l(k - 1)
                    p_lT(k - 1)
                if 2 <= k <= NB + 1:
                    p_ecT(k - 2)
                if 3 <= k <= NB + 2:
                    p_edT(k - 3)
                    p_slot(k - 3)

            pe.wait_ge(slot_sb, NB)
            pe.wait_ge(moe_in, 16 * (DC + 2 + EC * EPC))
            for e in range(E):
                q, p = e % 2, e // 2
                for k in range(DC):
                    mm = pe.matmul(PS[q * HID:(q + 1) * HID, p // 4, (p % 4) * P:(p % 4 + 1) * P], W1[:, k, e, :],
                                   SIN[:, k, e].rearrange("p b s -> p (b s)"), start=(k == 0), stop=(k == DC - 1))
                if q == 1:
                    mm.then_inc(hid_ps, 1)
            pe.wait_ge(hid_sb, EP)
            for k in range(DC):
                for p in range(EP):
                    for q in range(2):
                        bank = (2 + 4 * k + 2 * q + p // 4) % 8
                        mm = pe.matmul(PS[:, bank, (p % 4) * P:(p % 4 + 1) * P],
                                       W2[q * HID:(q + 1) * HID, p, k * P:(k + 1) * P], HS[q * HID:(q + 1) * HID, p, :],
                                       start=True, stop=True)
                mm.then_inc(so_ps, 1)
            pe.wait_ge(soa_sb, 4)
            pe.wait_ge(sov_sb, 4)

            def soT(b):
                if b >= 2:
                    pe.wait_ge(so_sb, b - 1)
                for k in range(EC):
                    for c in range(DC):
                        tr = pe.transpose(PS[:, 2 + b % 2, k * D + c * P:k * D + (c + 1) * P],
                                          SOT[:, c, b, k * EPC:(k + 1) * EPC, :].rearrange("p e s -> p (e s)"), ident[:])
                tr.then_inc(soT_ps, 1)

            def comb(b):
                pe.wait_ge(so_sb, b + 1)
                if b >= 2:
                    pe.wait_ge(y_sb, NC * (b - 1))
                for c in range(NC):
                    for k in range(EC):
                        mm = pe.matmul(PS[:, 4 + b % 2, c * D:(c + 1) * D], ECT[:, b, k, c * P:(c + 1) * P],
                                       SO[:, b % 2, k], start=(k == 0), stop=(k == EC - 1))
                mm.then_inc(y_ps, 1)

            soT(0)
            for b in range(NB):
                if b + 1 < NB:
                    soT(b + 1)
                comb(b)

        @block.vector
        def _(dve):
            def weights():
                dve.wait_ge(wT_ps, 7)
                dve.tensor_copy(WTA[:].rearrange("p k g -> p (k g)"), PS[:, 3, 0:96]).then_inc(wt_step, 1)
                dve.tensor_copy(B1[:], PS[:, 3, 96:96 + EP]).then_inc(b1_sb, 1)
                dve.wait_ge(wt_step, 1)
                dve.tensor_copy(WT[:, 0:2], WTA[:, 0:2]).then_inc(wt_step, 1)
                dve.tensor_tensor(WT[:, 2:4], WTA[:, 2:4], WTA[:, 4:6], ALU.add).then_inc(wt_step, 1)

            def stats(b):
                dve.wait_ge(x_in[b], 16)
                for t in (NC * b, NC * b + 1):
                    dve.bn_stats(ST[:, t], X[:, t]).then_inc(ln_st, 1)
                for t in (NC * b, NC * b + 1):
                    dve.wait_ge(ln_st, t + 1)
                    dve.bn_aggr(MV[:, t], ST[:, t]).then_inc(ln_mv, 1)

            def norm(b):
                dve.wait_ge(ln_rs, b + 1)
                for t in (NC * b, NC * b + 1):
                    dve.tensor_scalar(Q[:, t], X[:, t], MV[:, t, 0:1], RS[:, t:t + 1],
                                      ALU.subtract, ALU.mult).then_inc(q_sb, 1)
            stats(0)
            stats(1)
            for b in range(NB):
                if b + 2 < NB:
                    stats(b + 2)
                norm(b)
                if b == 0:
                    weights()
            dve.wait_ge(gate_ps, NT)
            dve.wait_ge(vec_in, 16 * 7)
            for g in range(2):
                dve.tensor_tensor(G1[:, g].rearrange("p c (b h) -> p b c h", h=H),
                                  PS[:, 2, 0:16 * NT].rearrange("p (b c g h) -> p g b c h", b=NB, c=NC, g=2)[:, g],
                                  BG[:, g].unsqueeze(1).unsqueeze(1).to_broadcast([P, NB, NC, H]),
                                  ALU.add).then_inc(gate_sb, 1)
            dve.wait_ge(gateT_ps, 1)
            IT = PS[0:BH, 4, 0:SEQ]
            dve.tensor_copy(FS[:], PS[0:BH, 4, SEQ:2 * SEQ]).then_inc(row_step, 1)
            dve.wait_ge(row_step, 1)
            dve.scalar_tensor_tensor(out=NA[:], in0=FS[:], scalar=-1.0, in1=FS[:], op0=ALU.mult,
                                     op1=ALU.min).then_inc(row_step, 1)
            dve.wait_ge(sig_l, 1)
            dve.scalar_tensor_tensor(out=LS[:], in0=FS[:], scalar=0.0, in1=LF[:], op0=ALU.min,
                                     op1=ALU.subtract).then_inc(row_step, 1)
            dve.wait_ge(row_step, 3)
            dve.tensor_tensor_scan(CS[:], ones[0:BH, 0:1].to_broadcast([BH, SEQ]), LS[:], 0.0,
                                   ALU.mult, ALU.add).then_inc(row_step, 1)
            dve.wait_ge(row_step, 4)
            dve.tensor_tensor(G[:], IT, CS[:], ALU.subtract).then_inc(row_step, 1)
            dve.wait_ge(row_step, 5)
            dve.tensor_tensor_scan(M[:], G[:], G[:], NEG_BIG, ALU.max, ALU.max).then_inc(row_step, 1)
            dve.wait_ge(row_step, 6)
            dve.tensor_scalar(NM[:], M[:], -1.0, None, ALU.mult).then_inc(row_step, 1)
            dve.tensor_tensor(CM[:], CS[:], M[:], ALU.add).then_inc(row_step, 1)
            dve.wait_ge(row_step, 8)
            dve.tensor_copy(MHL[:, 0], NM[:]).then_inc(split, 1)
            dve.tensor_copy(GHL[:, 0], G[:]).then_inc(split, 1)
            dve.wait_ge(split, 2)
            dve.tensor_tensor(MHL[:, 1], NM[:], MHL[:, 0].bitcast(F32), ALU.subtract).then_inc(split, 1)
            dve.tensor_tensor(GHL[:, 1], G[:], GHL[:, 0].bitcast(F32), ALU.subtract).then_inc(split, 1)
            dve.wait_ge(rowsT_ps, 1)
            dve.tensor_copy(TT[:].rearrange("p r n -> p (r n)"), PS[:, 5, 0:4 * BH]).then_inc(rowsT_sb, 1)
            dve.wait_ge(mu_sum, 1)
            dve.tensor_scalar(MUN[:], PS[:, 3, 0:ES], NORM_FLOOR_SQ, None, ALU.max).then_inc(mu_max, 1)
            dve.wait_ge(mu_sqrt, 1)
            dve.reciprocal(MUN[:], MUN[:]).then_inc(mu_step, 1)
            dve.wait_ge(mu_step, 1)
            dve.tensor_tensor(MU[:], MU[:], MUN[:].unsqueeze(1).to_broadcast([P, DC, ES]), ALU.mult).then_inc(mu_step, 1)

            def kv(b):
                dve.wait_ge(kv_ps, b + 1)
                if b >= 1:
                    dve.wait_ge(ho_ps, b)
                dve.tensor_tensor(KVS[:], PS[:, 7, 0:H * V1].rearrange("p (k v) -> p k v", k=2),
                                  blockmask[:].unsqueeze(1).to_broadcast([P, 2, HPC * V1]), ALU.mult).then_inc(kv_sb, 1)

            def cmul(b):
                dve.wait_ge(s_ps, b + 1)
                for c in range(NC):
                    dve.wait_ge(dec_mask, NC * b + c + 1)
                    d = DEC[:, b % 2, c].rearrange("p (k r) i -> p r k i", r=HPC)
                    dve.tensor_tensor(d, PS[:, 0:4, c * 256:(c + 1) * 256].rearrange("p r (k i) -> p r k i", k=2),
                                      d, ALU.mult).then_inc(c_sb, 1)

            def h1(b):
                u = b % 2
                f = TT[:, 3, H * b:H * b + H].unsqueeze(2).to_broadcast([P, H, V1])
                dve.wait_ge(ho_ps, b + 1)
                if b >= 1:
                    dve.wait_ge(h1_sb, b)
                dve.tensor_tensor(HT1[:], PS[:, 7, 0:H * V1].rearrange("p (h v) -> p h v", h=H), f,
                                  ALU.mult).then_inc(ho_sb, 1)
                dve.wait_ge(hd_ps, 2 * b + 2)
                dve.wait_ge(ho_sb, b + 1)
                dve.tensor_tensor(HB[:, u, 1], PS[:, 6, 0:H * V1].rearrange("p (h v) -> p h v", h=H), HT1[:],
                                  ALU.add).then_inc(h1_sb, 1)

            def post(b):
                u, st, B0 = b % 2, post_step, 12 * b
                hv = HB[:, u, :, :, 0:HD]

                def sm(i):
                    return SM[:, u, i].rearrange("p (c h) -> p c h", c=NC)

                def wide(i):
                    return sm(i).unsqueeze(3).to_broadcast([P, NC, H, HD]).rearrange("p c h v -> p (c h) v")
                dve.wait_ge(h1_sb, b + 1)
                dve.wait_ge(h0_sb, b + 1)
                dve.tensor_reduce(sm(0), hv, AX.X, ALU.add).then_inc(st, 1)
                dve.scalar_tensor_tensor(out=sm(1), in0=HB[:, u, :, :, HD], scalar=-1.0, in1=HB[:, u, :, :, HD],
                                         op0=ALU.mult, op1=ALU.max).then_inc(st, 1)
                dve.wait_ge(st, B0 + 2)
                dve.tensor_scalar(SM[:, u, 0], SM[:, u, 0], 1.0 / HD, None, ALU.mult).then_inc(st, 1)
                dve.scalar_tensor_tensor(out=sm(2), in0=TT[:, 0:2, H * b:H * b + H], scalar=TAU, in1=sm(1),
                                         op0=ALU.mult, op1=ALU.max).then_inc(st, 1)
                dve.wait_ge(st, B0 + 4)
                dve.tensor_scalar(SM[:, u, 2], SM[:, u, 2], TAU * 1e-6, None, ALU.add).then_inc(st, 1)
                if b >= 2:
                    dve.wait_ge(nrm_sb, b - 1)
                dve.wait_ge(st, B0 + 5)
                dve.reciprocal(SM[:, u, 3], SM[:, u, 2]).then_inc(st, 1)
                dve.tensor_tensor(HC[:, u].rearrange("p c h v -> p (c h) v"), hv.rearrange("p c h v -> p (c h) v"),
                                  wide(0), ALU.subtract).then_inc(st, 1)
                dve.wait_ge(st, B0 + 7)
                dve.tensor_tensor(SM[:, u, 4], SM[:, u, 3], SM[:, u, 3], ALU.mult).then_inc(st, 1)
                dve.wait_ge(sq_sb, b + 1)
                dve.tensor_reduce(sm(5), SQ[:], AX.X, ALU.add).then_inc(st, 1)
                dve.wait_ge(st, B0 + 9)
                dve.scalar_tensor_tensor(out=SM[:, u, 6], in0=SM[:, u, 5], scalar=1.0 / HD, in1=SM[:, u, 4],
                                         op0=ALU.mult, op1=ALU.mult).then_inc(st, 1)
                dve.wait_ge(gn_rs, b + 1)
                dve.tensor_tensor(SM[:, u, 9], SM[:, u, 8], SM[:, u, 3], ALU.mult).then_inc(st, 1)
                dve.wait_ge(st, B0 + 11)
                if b >= 2:
                    dve.wait_ge(x1_sb, b - 1)
                dve.tensor_copy(SM[:, u, 1], SM[:, u, 9]).then_inc(st, 1)
                dve.tensor_tensor(NRM[:, u].rearrange("p c (h v) -> p (c h) v", h=H),
                                  HC[:, u].rearrange("p c h v -> p (c h) v"), wide(9), ALU.mult).then_inc(nrm_sb, 1)

            kv(0)
            cmul(0)
            for b in range(NB):
                h1(b)
                if b + 1 < NB:
                    kv(b + 1)
                    cmul(b + 1)
                post(b)

            def lstats(b):
                dve.wait_ge(x1_sb, b + 1)
                for t in (NC * b, NC * b + 1):
                    dve.bn_stats(ST[:, t], Q[:, t]).then_inc(l_st, 1)
                for t in (NC * b, NC * b + 1):
                    dve.wait_ge(l_st, t + 1)
                    dve.bn_aggr(MV[:, t], ST[:, t]).then_inc(l_mv, 1)
                dve.wait_ge(l_mv, NC * (b + 1))
                dve.tensor_scalar(SS[:, b, 4], MV[:, NC * b:NC * b + NC, 1], 1.0 + LN_EPS, LN_EPS * LN_EPS,
                                  ALU.mult, ALU.add).then_inc(l_var, 1)

            def lnorm(b):
                dve.wait_ge(l_rs, b + 1)
                if b >= 2:
                    dve.wait_ge(xg_sb, b - 1)
                for c in range(NC):
                    t = NC * b + c
                    dve.tensor_scalar(XH[:, b % 2, c], Q[:, t], MV[:, t, 0:1], SS[:, b, 6, c:c + 1],
                                      ALU.subtract, ALU.mult).then_inc(xh_sb, 1)

            def cmax(b):
                dve.wait_ge(l_sb, NC * (b + 1))
                dve.tensor_reduce(SS[:, b, 7], LSB[:, b % 2], AX.X, ALU.max, negate=True).then_inc(rowmax_sb, 1)

            def dmax(b):
                dve.wait_ge(lT_ps, b + 1)
                dve.tensor_reduce(DM[:, b], PS[:, 2, :].rearrange("p (k n) -> p k n", k=EC), AX.X, ALU.max,
                                  negate=True).then_inc(colmax_sb, 1)

            def dnorm(b):
                dve.wait_ge(edt_sb, EC * (b + 1))
                dve.reciprocal(DR[:, b], DS[:, b]).then_inc(edt_step, 1)
                dve.wait_ge(edt_step, b + 1)
                for k in range(EC):
                    dve.tensor_scalar(EDT[:, b % 2, k], EDT[:, b % 2, k], DR[:, b, k:k + 1], None,
                                      ALU.mult).then_inc(edt_n, 1)

            def ecT(b):
                dve.wait_ge(ecT_ps, b + 1)
                dve.tensor_copy(ECT[:, b].rearrange("p k n -> p (k n)"), PS[:, 4, :]).then_inc(ecT_sb, 1)

            def edc(b):
                dve.wait_ge(edT_ps, b + 1)
                if b >= 2:
                    dve.wait_ge(slot_ps, b - 1)
                dve.tensor_copy(ED[:, b % 2].rearrange("p c e -> p (c e)"), PS[:, 3, :]).then_inc(ed_sb, 1)

            lstats(0)
            for k in range(-1, NB + 4):
                if 0 <= k + 2 < NB and k + 2 >= 1:
                    lstats(k + 2)
                if 0 <= k + 1 < NB:
                    lnorm(k + 1)
                if 1 <= k <= NB:
                    cmax(k - 1)
                    dmax(k - 1)
                if 2 <= k <= NB + 1:
                    dnorm(k - 2)
                    ecT(k - 2)
                if 3 <= k <= NB + 2:
                    edc(k - 3)
            dve.wait_ge(ec_sb, NT)
            dve.reciprocal(RCI[:], RC[:]).then_inc(rc_sb, 1)

            for k in range(DC):
                dve.wait_ge(so_ps, k + 1)
                for pp in range(2):
                    bank = (2 + 4 * k + 2 + pp) % 8
                    dve.tensor_copy(SOT[:, k, :, 8 * pp + 1:8 * pp + 8:2, :].rearrange("p b e s -> p e b s"),
                                    PS[:, bank, :].rearrange("p (e b s) -> p e b s", e=4, b=NB)).then_inc(sov_sb, 1)

            def so(b):
                dve.wait_ge(soT_ps, b + 1)
                if b >= 2:
                    dve.wait_ge(y_ps, b - 1)
                if b == 0:
                    dve.wait_ge(moe_in, 16 * (DC + 2 + EC * EPC))
                dve.tensor_tensor(SO[:, b % 2], PS[:, 2 + b % 2, :].rearrange("p (k d) -> p k d", k=EC), B2R[:],
                                  ALU.add).then_inc(so_sb, 1)

            def yy(b):
                dve.wait_ge(y_ps, b + 1)
                if b >= 2:
                    dve.wait_ge(y_out[b % 2], 16 * (b // 2))
                if b == 0:
                    dve.wait_ge(rc_sb, 1)
                for c in range(NC):
                    dve.scalar_tensor_tensor(out=Y[:, b % 2, c], in0=PS[:, 4 + b % 2, c * D:(c + 1) * D],
                                             scalar=RCI[:, b, c:c + 1], in1=Q[:, NC * b + c], op0=ALU.mult,
                                             op1=ALU.add).then_inc(y_sb, 1)
            so(0)
            for b in range(NB):
                if b + 1 < NB:
                    so(b + 1)
                yy(b)


_INS = ['x', 'ctx_1024', 'L0_xattn_Wi_w', 'L0_xattn_Wi_b', 'L0_xattn_Wf_w', 'L0_xattn_Wf_b', 'L0_xattn_gn_w',
        'L0_xattn_gn_b', 'L0_ffn_ln_gamma', 'L0_ffn_ln_beta', 'L0_ffn_mu', 'L0_ffn_scale', 'L0_ffn_w1',
        'L0_ffn_b1', 'L0_ffn_w2', 'L0_ffn_b2']


def kernel(**inputs):
    import concourse.bacc as _bacc
    from concourse.bass_utils import run_bass_kernel_spmd as _run

    nc = _bacc.Bacc("TRN2", target_bir_lowering=False, num_devices=1)
    arrays, args = {}, []
    for name in _INS:
        a = np.ascontiguousarray(inputs[name])
        arrays[f"in_{name}"] = a
        args.append(nc.dram_tensor(f"in_{name}", a.shape, mybir.dt.from_np(a.dtype), kind="ExternalInput").ap())
    y = nc.dram_tensor("out_0", tuple(inputs['x'].shape), F32, kind="ExternalOutput").ap()
    xattn_ffn(nc, *args, y)
    r = _run(nc, [arrays], core_ids=[0])
    return r.results[0]["out_0"]
```

```python
from contextlib import ExitStack

import numpy as np

import concourse.bass as bass
from concourse import mybir

F32 = mybir.dt.float32
F32R = mybir.dt.float32r
ALU = mybir.AluOpType
ACT = mybir.ActivationFunctionType
AX = mybir.AxisListType

P = 128
TAU = 32.0 ** 0.5
LN_EPS = 1e-5
NORM_FLOOR_SQ = 1e-24
NEG_BIG = -3.0e38


def xattn_ffn(nc, x, ctx_in, Wi_w, Wi_b, Wf_w, Wf_b, gn_w, gn_b,
              ln_gamma, ln_beta, mu, scale, w1, b1, w2, b2, out):
    NB, SEQ, D = x.shape
    H = Wi_w.shape[0]
    HD = D // H
    V1 = HD + 1
    NC = SEQ // P
    NT = NB * NC
    _, E, S = mu.shape
    HID = w1.shape[2]
    ES = E * S
    DC = D // P
    EC = ES // P
    EP = E // 2
    BH = NB * H
    HPC = P // HD
    EPC = P // S
    assert NC == 2 and DC == 2 and EC == 2 and H == 8 and HID == 64 and NB * S == P

    with ExitStack() as stack:
        def sb(name, shape, dt=F32):
            return stack.enter_context(nc.sbuf_tensor(name, shape, dt))

        def sem(name):
            return stack.enter_context(nc.semaphore(name))

        X = sb("X", [P, NT, D])
        CX = [sb("C0", [P, NB, D]), sb("C1", [P, NB, D])]
        D0 = sb("D0", [P, NC * H * P])
        DEC = [D0[:].rearrange("p (c h i) -> p c h i", c=NC, h=H),
               CX[1][:].rearrange("p b d -> p (b d)").rearrange("p (c h i) -> p c h i", c=NC, h=H)]
        SIN = [v.rearrange("p c h i -> p (c h i)").rearrange("p (e b s) -> p e b s", e=E, b=NB) for v in DEC]
        VE = sb("VE", [P, NT, H, V1])
        ECT = VE[:].rearrange("p t h v -> p (t h v)")[:, 0:NB * EC * SEQ].rearrange(
            "p (b k n) -> p b k n", b=NB, k=EC)
        Q = sb("Q", [P, NT, D])
        QKT = sb("QKT", [P, NT, 2 * DC, P])
        flat = QKT[:].rearrange("p t k n -> p (t k n)")
        W = NC * D
        XN = flat[:, 0:6 * W].rearrange("p (u c d) -> p u c d", u=6, c=NC)
        XNT = flat[:, 6 * W:8 * W].rearrange("p (u k n) -> p u k n", u=2, k=DC)
        LSB = flat[:, 8 * W:10 * W].rearrange("p (u c e) -> p u c e", u=2, c=NC)
        ECB = flat[:, 10 * W:12 * W].rearrange("p (u c e) -> p u c e", u=2, c=NC)
        EDT = flat[:, 12 * W:14 * W].rearrange("p (u k n) -> p u k n", u=2, k=EC)
        ED = flat[:, 14 * W:16 * W].rearrange("p (u c e) -> p u c e", u=2, c=NC)
        SOT = flat[:, 0:8 * W].rearrange("p (k b e s) -> p k b e s", k=DC, b=NB, e=E)
        SO = flat[:, 8 * W:10 * W].rearrange("p (u k d) -> p u k d", u=2, k=EC)
        Y = flat[:, 10 * W:12 * W].rearrange("p (u c d) -> p u c d", u=2, c=NC)
        HPB = flat[:, 12 * W:14 * W].rearrange("p (e n) -> p e n", e=EP)
        QZ = sb("QZ", [P, 2, NC, DC, HPC, P])
        HSZ = QZ[:, 0].rearrange("p c k r i -> p (c k r i)").rearrange("p (e q n) -> p e q n", e=EP, q=2)
        MROW = sb("MROW", [4, H, SEQ], F32R)
        GROW = sb("GROW", [4, H, SEQ], F32R)
        MHL = sb("MHL", [BH, 2, SEQ], F32R)
        GHL = sb("GHL", [BH, 2, SEQ], F32R)
        ident = sb("ident", [P, P])
        ones = sb("ones", [P, P])
        blockmask = sb("blockmask", [P, HPC * V1])
        neghalf = sb("neghalf", [P, NC * H])
        GNW = sb("GNW", [P, D])
        GNB = sb("GNB", [P, D])
        GAM = sb("GAM", [P, D])
        BET = sb("BET", [P, D])
        SCL = sb("SCL", [P, 1])
        BG = sb("BG", [P, 1])
        WW = sb("WW", [2 * H, 3 * D])
        WTA = sb("WTA", [P, 6, 2 * H])
        WZ = sb("WZ", [P, 4, 2 * BH + BH - H])
        B1L = sb("B1L", [EP, P])
        B1 = sb("B1", [P, EP])
        B2R = sb("B2R", [P, EC, D])
        W1 = sb("W1", [P, DC, E, HID])
        W2 = sb("W2", [P, EP, D])
        MU = sb("MU", [P, DC, ES])
        MUN = sb("MUN", [P, ES])
        ST = sb("ST", [P, NT, 6])
        MV = sb("MV", [P, NT, 2])
        LV = sb("LV", [P, NT])
        RS = sb("RS", [P, NT])
        VM = sb("VM", [P, NT, H])
        FS = sb("FS", [BH, SEQ])
        NA = sb("NA", [BH, SEQ])
        EF = sb("EF", [BH, SEQ])
        LF = sb("LF", [BH, SEQ])
        LS = sb("LS", [BH, SEQ])
        CS = sb("CS", [BH, SEQ])
        G = sb("G", [BH, SEQ])
        M = sb("M", [BH, SEQ])
        NM = sb("NM", [BH, SEQ])
        CM = sb("CM", [BH, SEQ])
        ROWS = sb("ROWS", [BH, 4, P])
        TT = sb("TT", [P, 4, BH])
        EK = sb("EK", [P, 2, H, HD])
        KVS = sb("KVS", [P, 2, HPC * V1])
        HT1 = sb("HT1", [P, H, V1])
        HB = sb("HB", [P, 2, NC, H, V1])
        SQ = sb("SQ", [P, NC, H, HD])
        SM = sb("SM", [P, 2, 10, NC * H])
        NRM = sb("NRM", [P, 2, NC, D])
        XH = NRM
        MUQ = NRM[:, 0]
        JNK = SQ[:, 0].rearrange("p h v -> p (h v)")
        SS = sb("SS", [P, NB, 8, NC])
        RC = sb("RC", [P, NB, NC])
        RCI = sb("RCI", [P, NB, NC])
        DM = sb("DM", [P, NB, EC])
        DS = sb("DS", [P, NB, EC])
        DR = sb("DR", [P, NB, EC])
        PS = stack.enter_context(nc.psum_tensor("PS", [P, 8, 512], F32))

        x_in = [sem(f"x_in{b}") for b in range(NB)]
        c_in = [sem(f"c_in{b}") for b in range(NB)]
        w_in = sem("w_in")
        mu_in = sem("mu_in")
        vec_in = sem("vec_in")
        moe_in = sem("moe_in")

        rows_in = sem("rows_in")
        qz_in = [sem("qz_in0"), sem("qz_in1")]
        y_out = [sem("y_out0"), sem("y_out1")]
        consts = sem("consts")
        const_step = sem("const_step")
        wT_ps = sem("wT_ps")
        wt_step = sem("wt_step")
        b1_sb = sem("b1_sb")
        musq = sem("musq")
        mu_sum = sem("mu_sum")
        mu_max = sem("mu_max")
        mu_sqrt = sem("mu_sqrt")
        mu_step = sem("mu_step")
        ln_st = sem("ln_st")
        ln_mv = sem("ln_mv")
        ln_var = sem("ln_var")
        ln_rs = sem("ln_rs")
        q_sb = sem("q_sb")
        qk_ps = sem("qk_ps")
        qk_sb = sem("qk_sb")
        ve_ones = sem("ve_ones")
        v_sum = sem("v_sum")
        v_mean = sem("v_mean")
        rows_one = sem("rows_one")
        qz_zero = sem("qz_zero")
        wz_zero = sem("wz_zero")
        hs_zero = sem("hs_zero")
        hpb_sb = sem("hpb_sb")
        ve_sb = sem("ve_sb")
        gate_ps = sem("gate_ps")
        row_step = sem("row_step")
        sig_e = sem("sig_e")
        sig_l = sem("sig_l")
        tok_rows = sem("tok_rows")
        split = sem("split")
        rowsT_ps = sem("rowsT_ps")
        rowsT_sb = sem("rowsT_sb")
        arg_ps = sem("arg_ps")
        dec_sb = sem("dec_sb")
        dec_mask = sem("dec_mask")
        s_ps = sem("s_ps")
        c_sb = sem("c_sb")
        ek_sb = sem("ek_sb")
        kv_ps = sem("kv_ps")
        kv_sb = sem("kv_sb")
        ho_ps = sem("ho_ps")
        ho_sb = sem("ho_sb")
        hd_ps = sem("hd_ps")
        h0_sb = sem("h0_sb")
        h1_sb = sem("h1_sb")
        post_step = sem("post_step")
        sq_sb = sem("sq_sb")
        gn_var = sem("gn_var")
        gn_rs = sem("gn_rs")
        nrm_sb = sem("nrm_sb")
        xb_sb = sem("xb_sb")
        gw_sb = sem("gw_sb")
        x1_sb = sem("x1_sb")
        l_st = sem("l_st")
        l_mv = sem("l_mv")
        l_var = sem("l_var")
        l_rs = sem("l_rs")
        xh_sb = sem("xh_sb")
        xg_sb = sem("xg_sb")
        xn_sb = sem("xn_sb")
        ss_sb = sem("ss_sb")
        rn_step = sem("rn_step")
        rn_sb = sem("rn_sb")
        xnT_ps = sem("xnT_ps")
        xnT_sb = sem("xnT_sb")
        l_ps = sem("l_ps")
        l_sb = sem("l_sb")
        rowmax_sb = sem("rowmax_sb")
        ec_sb = sem("ec_sb")
        lT_ps = sem("lT_ps")
        colmax_sb = sem("colmax_sb")
        edt_sb = sem("edt_sb")
        edt_step = sem("edt_step")
        edt_n = sem("edt_n")
        edT_ps = sem("edT_ps")
        ed_sb = sem("ed_sb")
        ecT_ps = sem("ecT_ps")
        ecT_sb = sem("ecT_sb")
        rc_sb = sem("rc_sb")
        slot_ps = sem("slot_ps")
        slot_sb = sem("slot_sb")
        hid_ps = sem("hid_ps")
        hid_sb = sem("hid_sb")
        so_ps = sem("so_ps")
        soa_sb = sem("soa_sb")
        sov_sb = sem("sov_sb")
        soT_ps = sem("soT_ps")
        so_sb = sem("so_sb")
        y_ps = sem("y_ps")
        y_sb = sem("y_sb")

        block = stack.enter_context(nc.Block())

        NVEC = 2 * NB + 5

        @block.sync
        def _(sp):
            def bc(v, n=P):
                return v.partition_broadcast(n)

            def tok(a, b):
                return a[b].rearrange("(c p) d -> p c d", p=P)
            def load(b):
                sp.dma_start(X[:, NC * b:NC * b + NC, :], tok(x, b)).then_inc(x_in[b], 16)
                for c in range(NC):
                    sp.dma_start(CX[c][:, b, :], ctx_in[b, c * P:(c + 1) * P, :]).then_inc(c_in[b], 16)
            load(0)
            sp.dma_start(WW[0:H, :], Wi_w).then_inc(w_in, 16)
            sp.dma_start(WW[H:2 * H, :], Wf_w).then_inc(w_in, 16)
            sp.dma_start(B1L[:], b1.rearrange("(p q) h -> p (q h)", q=2)).then_inc(w_in, 16)
            load(1)
            sp.dma_start(MU[:], mu.rearrange("(k p) e s -> p k (e s)", p=P)).then_inc(mu_in, 16)
            for b in range(2, NB):
                load(b)

            def head_copies(b):
                for i in range(HPC):
                    rows = slice(HD * i, HD * i + HD)
                    for c in range(NC):
                        sp.dma_start(QZ[rows, b % 2, c, :, i, :], QKT[rows, NC * b + c, 0:DC, :]).then_inc(qz_in[b % 2], 16)
            for g, v in ((0, Wi_b), (1, Wf_b)):
                for b in range(NB):
                    sp.dma_start(BG[g * BH + H * b:g * BH + H * b + H, 0:1], v.unsqueeze(1)).then_inc(vec_in, 16)
            sp.wait_ge(qz_zero, 2)
            for b in range(2):
                sp.wait_ge(qk_sb, NC * (b + 1))
                head_copies(b)
            sp.dma_start(GNW[:], bc(gn_w)).then_inc(vec_in, 16)
            sp.dma_start(GNB[:], bc(gn_b)).then_inc(vec_in, 16)
            sp.dma_start(GAM[:], bc(ln_gamma)).then_inc(vec_in, 16)
            sp.dma_start(BET[:], bc(ln_beta)).then_inc(vec_in, 16)
            sp.dma_start(SCL[:], bc(scale)).then_inc(vec_in, 16)
            sp.wait_ge(rows_one, 2)
            sp.wait_ge(split, 4)
            for b in range(NB):
                if b >= 1:
                    sp.wait_ge(arg_ps, 4 * b)
                for a in range(2):
                    sp.dma_start(MROW[a:a + 1].bitcast(F32), MHL[H * b:H * b + H, a, :].bitcast(F32)).then_inc(rows_in, 16)
                    sp.dma_start(GROW[2 + a:3 + a].bitcast(F32), GHL[H * b:H * b + H, a, :].bitcast(F32)).then_inc(rows_in, 16)
                if b == 0:
                    for k in range(DC):
                        sp.dma_start(W1[:, k], w1[:, k * P:(k + 1) * P, :].rearrange("e p h -> p e h")).then_inc(moe_in, 16)
                    for q in range(2):
                        sp.dma_start(W2[q * HID:(q + 1) * HID], w2.rearrange("(p q) h d -> q h p d", q=2)[q]).then_inc(moe_in, 16)
                if b == 1:
                    for k in range(EC):
                        for e in range(EPC):
                            sp.dma_start(B2R[e * S:(e + 1) * S, k, :], bc(b2[k * EPC + e], S)).then_inc(moe_in, 16)
                if 1 <= b < NB - 1:
                    sp.wait_ge(s_ps, NC * b)
                    head_copies(b + 1)
            for b in range(NB):
                sp.wait_ge(y_sb, NC * (b + 1))
                sp.dma_start(out[b].rearrange("(c p) d -> p c d", p=P), Y[:, b % 2]).then_inc(y_out[b % 2], 16)
            sp.wait_ge(y_out[0], 16 * (NB // 2))
            sp.wait_ge(y_out[1], 16 * (NB // 2))

        @block.gpsimd
        def _(pool):
            def centre(b):
                pool.wait_ge(v_mean, b + 1)
                for c in range(NC):
                    pool.tensor_tensor(VE[:, NC * b + c, :, 0:HD], CX[c][:, b].rearrange("p (h v) -> p h v", h=H),
                                       VM[:, NC * b + c].unsqueeze(2).to_broadcast([P, H, HD]),
                                       ALU.subtract).then_inc(ve_sb, 1)

            def residual(b):
                xb = X[:, NC * b:NC * b + NC, :]
                pool.tensor_tensor(xb, xb, GNB[:].unsqueeze(1).to_broadcast([P, NC, D]), ALU.add).then_inc(xb_sb, 1)

            pool.memset(ident[:], 1.0).then_inc(const_step, 1)
            pool.memset(ones[:], 1.0).then_inc(consts, 1)
            pool.memset(blockmask[:], 1.0).then_inc(const_step, 1)
            pool.memset(neghalf[:], -0.5).then_inc(consts, 1)
            pool.wait_ge(const_step, 2)
            pool.affine_select(out=ident[:], in_=ident[:], compare_op=ALU.is_equal, fill=0.0, base=0,
                               pattern=[[-1, P]], channel_multiplier=1).then_inc(consts, 1)
            pool.wait_ge(consts, 3)
            pool.memset(VE[:, :, :, HD:V1], 1.0).then_inc(ve_ones, 1)
            for b in range(NB):
                t = NC * b
                pool.wait_ge(ln_mv, t + NC)
                pool.tensor_scalar(LV[:, t:t + NC], MV[:, t:t + NC, 1], 1.0, LN_EPS, ALU.mult, ALU.add).then_inc(ln_var, 1)
                pool.wait_ge(ln_var, b + 1)
                pool.tensor_tensor(RS[:, t:t + NC], LV[:, t:t + NC], neghalf[:, 0:NC], ALU.pow).then_inc(ln_rs, 1)
                if b == 0:
                    pool.memset(QZ[:, 0], 0.0).then_inc(qz_zero, 1)
                    pool.wait_ge(mu_in, 16)
                    pool.tensor_tensor(MUQ, MU[:], MU[:], ALU.mult).then_inc(musq, 1)
                if b == 1:
                    pool.memset(QZ[:, 1], 0.0).then_inc(qz_zero, 1)
                if b >= 1:
                    centre(b - 1)
            centre(NB - 1)
            bm = blockmask[:].rearrange("p (r v) -> p r v", r=HPC)
            pool.affine_select(out=bm, in_=bm, compare_op=ALU.is_ge, fill=0.0, base=0,
                               pattern=[[-HD, HPC], [0, V1]], channel_multiplier=1).then_inc(const_step, 1)
            pool.wait_ge(const_step, 3)
            pool.affine_select(out=bm, in_=bm, compare_op=ALU.is_gt, fill=0.0, base=HD,
                               pattern=[[HD, HPC], [0, V1]], channel_multiplier=-1).then_inc(const_step, 1)
            pool.memset(MROW[:].bitcast(F32), 1.0).then_inc(rows_one, 1)
            pool.memset(GROW[:].bitcast(F32), 1.0).then_inc(rows_one, 1)
            pool.wait_ge(q_sb, NT)
            pool.wait_ge(vec_in, 16 * NVEC)
            for b in range(NB // 2):
                residual(b)

            def ev(b):
                if b == 0:
                    pool.wait_ge(rowsT_sb, 1)
                if b >= 2:
                    pool.wait_ge(kv_ps, b - 1)
                e = TT[:, 2, H * b:H * b + H].unsqueeze(2).to_broadcast([P, H, HD])
                pool.tensor_tensor(EK[:, b % 2], CX[0][:, b].rearrange("p (h v) -> p h v", h=H), e, ALU.mult).then_inc(ek_sb, 1)

            def masks(b):
                for c in range(NC):
                    pool.wait_ge(dec_sb, 4 * b + 2 * c + 2)
                    d = DEC[b % 2][:, c]
                    pool.affine_select(out=d, in_=d, compare_op=ALU.is_ge, fill=0.0, base=0,
                                       pattern=[[0, H], [1, P]], channel_multiplier=-1).then_inc(dec_mask, 1)

            def head_rs(b):
                u = b % 2
                pool.wait_ge(post_step, 8 * b + 7)
                pool.tensor_scalar(SM[:, u, 7], SM[:, u, 6], 1.0, LN_EPS, ALU.mult, ALU.add).then_inc(gn_var, 1)
                pool.wait_ge(gn_var, b + 1)
                pool.tensor_tensor(SM[:, u, 8], SM[:, u, 7], neghalf[:], ALU.pow).then_inc(gn_rs, 1)

            ev(0)
            for b in range(NB + 1):
                if b < NB:
                    masks(b)
                    if b + 1 < NB:
                        ev(b + 1)
                if b >= 1:
                    head_rs(b - 1)
                if 1 <= b <= NB // 2:
                    residual(NB // 2 + b - 1)

            def affine(b):
                u = b % 2
                pool.wait_ge(xh_sb, NC * (b + 1))
                if b >= 6:
                    pool.wait_ge(slot_ps, b - 5)
                if b == 0:
                    pool.wait_ge(hd_ps, 2 * NB)
                    pool.wait_ge(ho_ps, NB)
                pool.tensor_tensor(XN[:, b % 6], XH[:, u], GAM[:].unsqueeze(1).to_broadcast([P, NC, D]),
                                   ALU.mult).then_inc(xg_sb, 1)
                pool.wait_ge(xg_sb, b + 1)
                pool.tensor_tensor(XN[:, b % 6], XN[:, b % 6], BET[:].unsqueeze(1).to_broadcast([P, NC, D]),
                                   ALU.add).then_inc(xn_sb, 1)

            def norm(b):
                pool.wait_ge(ss_sb, NC * (b + 1))
                pool.tensor_scalar(SS[:, b, 1], SS[:, b, 0], NORM_FLOOR_SQ, 0.0, ALU.max, ALU.add).then_inc(rn_step, 1)
                pool.wait_ge(rn_step, 2 * b + 1)
                pool.tensor_tensor(SS[:, b, 2], SS[:, b, 1], neghalf[:, 0:NC], ALU.pow).then_inc(rn_step, 1)
                pool.wait_ge(rn_step, 2 * b + 2)
                pool.tensor_tensor(SS[:, b, 3], SS[:, b, 2], SCL[:].to_broadcast([P, NC]), ALU.mult).then_inc(rn_sb, 1)

            def lnrs(b):
                pool.wait_ge(l_var, b + 1)
                pool.tensor_tensor(SS[:, b, 6], SS[:, b, 4], neghalf[:, 0:NC], ALU.pow).then_inc(l_rs, 1)

            lnrs(0)
            affine(0)
            lnrs(1)
            pool.memset(HSZ, 0.0).then_inc(hs_zero, 1)
            for k in range(NB):
                if k + 1 < NB:
                    affine(k + 1)
                norm(k)
                if k + 2 < NB:
                    lnrs(k + 2)

        @block.scalar
        def _(act):
            def qk_copy(t):
                act.wait_ge(qk_ps, t + 1)
                act.copy(QKT[:, t].rearrange("p k n -> p (k n)"), PS[:, t % 2, :]).then_inc(qk_sb, 1)
            qk_copy(0)
            qk_copy(1)
            qk_copy(2)
            qk_copy(3)
            act.wait_ge(mu_max, 1)
            act.activation(MUN[:], MUN[:], ACT.Sqrt).then_inc(mu_sqrt, 1)
            for t in range(4, NT):
                qk_copy(t)
            act.wait_ge(row_step, 2)
            act.activation(EF[:], NA[:], ACT.Exp).then_inc(sig_e, 1)
            act.wait_ge(sig_e, 1)
            act.activation(LF[:], EF[:], ACT.Ln, bias=ones[0:BH, 0:1]).then_inc(sig_l, 1)
            act.wait_ge(row_step, 8)
            act.activation(ROWS[:, 2, :], G[:, 0:P], ACT.Exp, bias=NM[:, P - 1:P]).then_inc(tok_rows, 1)
            act.activation(ROWS[:, 3, :], NM[:, P:SEQ], ACT.Exp, bias=M[:, P - 1:P]).then_inc(tok_rows, 1)
            act.activation(ROWS[:, 0:2, :], CM[:].rearrange("r (c i) -> r c i", c=NC), ACT.Exp,
                           scale=-1.0).then_inc(tok_rows, 1)

            def decay(b, lo, hi):
                for k in range(4 * b + lo, 4 * b + hi):
                    c, half = (k // 2) % 2, k % 2
                    act.wait_ge(arg_ps, k + 1)
                    if b == 1 and k == 4:
                        act.wait_ge(ve_sb, NT)
                    if b >= 2:
                        act.wait_ge(hd_ps, 2 * (b - 2) + 2)
                    act.activation(DEC[b % 2][:, c, 4 * half:4 * half + 4, :],
                                   PS[:, 4 + k % 2, :].rearrange("p (h i) -> p h i", h=4),
                                   ACT.Exp).then_inc(dec_sb, 1)

            def h0(b):
                act.wait_ge(hd_ps, 2 * b + 1)
                if b >= 2:
                    act.wait_ge(nrm_sb, b - 1)
                act.copy(HB[:, b % 2, 0], PS[:, 6, 0:H * V1].rearrange("p (h v) -> p h v", h=H)).then_inc(h0_sb, 1)

            def squares(b):
                act.wait_ge(h1_sb, b + 1)
                act.wait_ge(h0_sb, b + 1)
                if b >= 1:
                    act.wait_ge(post_step, 8 * (b - 1) + 6)
                act.activation(SQ[:], HB[:, b % 2, :, :, 0:HD], ACT.Square).then_inc(sq_sb, 1)

            decay(0, 0, 4)
            for b in range(NB):
                if b + 1 < NB:
                    decay(b + 1, 0, 2)
                h0(b)
                if b + 1 < NB:
                    decay(b + 1, 2, 4)
                squares(b)

            def sqn(b):
                act.wait_ge(xn_sb, b + 1)
                for c in range(NC):
                    if b or c:
                        act.wait_ge(ss_sb, NC * b + c)
                    act.activation(JNK[:], XN[:, b % 6, c], ACT.Square, accum_out=SS[:, b, 0, c:c + 1]).then_inc(ss_sb, 1)

            def xnt(b):
                act.wait_ge(xnT_ps, b + 1)
                if b >= 2:
                    act.wait_ge(l_ps, b - 1)
                act.copy(XNT[:, b % 2].rearrange("p k n -> p (k n)"), PS[:, 0, :]).then_inc(xnT_sb, 1)

            def lsb(b):
                act.wait_ge(l_ps, b + 1)
                act.wait_ge(rn_sb, b + 1)
                if b >= 2:
                    act.wait_ge(lT_ps, b - 1)
                for c in range(NC):
                    act.activation(LSB[:, b % 2, c], PS[:, 1, c * ES:(c + 1) * ES], ACT.Copy,
                                   scale=SS[:, b, 3, c:c + 1]).then_inc(l_sb, 1)

            def ecb(b):
                act.wait_ge(rowmax_sb, b + 1)
                if b >= 2:
                    act.wait_ge(ecT_ps, b - 1)
                for c in range(NC):
                    act.activation(ECB[:, b % 2, c], LSB[:, b % 2, c], ACT.Exp, bias=SS[:, b, 7, c:c + 1],
                                   accum_out=RC[:, b, c:c + 1]).then_inc(ec_sb, 1)

            def edt(b):
                act.wait_ge(colmax_sb, b + 1)
                if b >= 2:
                    act.wait_ge(edT_ps, b - 1)
                for k in range(EC):
                    act.activation(EDT[:, b % 2, k], PS[:, 2, k * SEQ:(k + 1) * SEQ], ACT.Exp,
                                   bias=DM[:, b, k:k + 1], accum_out=DS[:, b, k:k + 1]).then_inc(edt_sb, 1)

            def slot(b):
                act.wait_ge(slot_ps, b + 1)
                if b == 0:
                    act.wait_ge(hd_ps, 2 * NB)
                for k in range(DC):
                    act.copy(SIN[k][:, :, b, :], PS[:, 5, k * ES:(k + 1) * ES].rearrange("p (e s) -> p e s", e=E)).then_inc(slot_sb, 1)

            for k in range(NB + 5):
                if 3 <= k <= NB + 2:
                    edt(k - 3)
                if 2 <= k <= NB + 1:
                    ecb(k - 2)
                if k < NB:
                    xnt(k)
                    sqn(k)
                if 5 <= k:
                    slot(k - 5)
                if 1 <= k <= NB:
                    lsb(k - 1)
            for h in range(2):
                act.wait_ge(hpb_sb, h + 1)
                if h == 0:
                    act.wait_ge(hs_zero, 1)
                for q in range(2):
                    rows = slice(q * HID, q * HID + HID)
                    act.activation(HSZ[rows, 4 * h:4 * h + 4, q, :], HPB[rows, 4 * h:4 * h + 4, :],
                                   ACT.Gelu).then_inc(hid_sb, 1)
            for k in range(DC):
                act.wait_ge(so_ps, 2 * k + 2)
                for g in range(2):
                    act.copy(SOT[:, k, :, 4 * g:4 * g + 4, :].rearrange("p b e s -> p e b s"),
                             PS[:, (2 + 4 * k + g) % 8, :].rearrange("p (e b s) -> p e b s", e=4, b=NB)).then_inc(soa_sb, 1)

        @block.tensor
        def _(pe):
            pe.wait_ge(consts, 3)

            def qk_transposes(t):
                b, c = t // NC, t % NC
                pe.wait_ge(q_sb, t + 1)
                pe.wait_ge(c_in[b], 16 * NC)
                if t >= 2:
                    pe.wait_ge(qk_sb, t - 1)
                for k in range(DC):
                    pe.transpose(PS[:, t % 2, k * P:(k + 1) * P], Q[:, t, k * P:(k + 1) * P], ident[:])
                for k in range(DC):
                    tr = pe.transpose(PS[:, t % 2, (DC + k) * P:(DC + k + 1) * P], CX[c][:, b, k * P:(k + 1) * P], ident[:])
                tr.then_inc(qk_ps, 1)

            def gates(b):
                pe.wait_ge(qk_sb, NC * (b + 1))
                for k in range(4):
                    mm = pe.matmul(PS[:, 2, 0:SEQ], WZ[:, k, BH - H - H * b:BH - H - H * b + 2 * BH],
                                   QKT[:, NC * b:NC * b + NC, k, :], start=(b == 0 and k == 0),
                                   stop=(b == NB - 1 and k == 3))
                mm.then_inc(gate_ps, 1)

            pe.wait_ge(w_in, 48)
            for k in range(6):
                pe.transpose(PS[:, 3, k * 16:(k + 1) * 16], WW[:, k * P:(k + 1) * P], ident[0:16, 0:16])
            pe.transpose(PS[:, 3, 96:96 + EP], B1L[:], ident[0:EP, 0:EP]).then_inc(wT_ps, 1)
            qk_transposes(0)
            qk_transposes(1)
            qk_transposes(2)
            qk_transposes(3)
            pe.wait_ge(musq, 1)
            pe.wait_ge(b1_sb, 1)
            for k in range(DC):
                mm = pe.matmul(PS[:, 3, 0:ES], ones[:], MUQ[:, k], start=(k == 0), stop=(k == DC - 1))
            mm.then_inc(mu_sum, 1)
            pe.wait_ge(wt_step, 3)
            for b in range(2, NB):
                gates(b - 2)
                qk_transposes(NC * b)
                qk_transposes(NC * b + 1)
            gates(NB - 2)
            gates(NB - 1)

            def args(b, lo, hi):
                if lo == 0:
                    pe.wait_ge(rows_in, 64 * (b + 1))
                for k in range(4 * b + lo, 4 * b + hi):
                    c, half = (k // 2) % 2, k % 2
                    if k >= 2:
                        pe.wait_ge(dec_sb, k - 1)
                    elif k == 1:
                        pe.wait_ge(rowsT_sb, 1)
                    for j in range(4):
                        h = 4 * half + j
                        mm = pe.matmul(PS[:, 4 + k % 2, j * P:(j + 1) * P], GROW[0:4, h, c * P:(c + 1) * P],
                                       MROW[0:4, h, c * P:(c + 1) * P], start=True, stop=True)
                    mm.then_inc(arg_ps, 1)

            def scores(b, c):
                if c == 0:
                    pe.wait_ge(qz_in[b % 2], 16 * HPC * NC * (b // 2 + 1))
                if b == 0:
                    pe.wait_ge(qk_sb, NT)
                    pe.wait_ge(mu_max, 1)
                    if c == 1:
                        pe.wait_ge(row_step, 5)
                if b >= 1:
                    pe.wait_ge(c_sb, NC * (b - 1) + c + 1)
                for hh in range(DC):
                    mm = pe.matmul(PS[:, 2 * c + hh, :], QKT[:, NC * b + c, DC + hh, :],
                                   QZ[:, b % 2, c, hh].rearrange("p r i -> p (r i)"), start=True, stop=True)
                mm.then_inc(s_ps, 1)

            def state(b):
                pe.wait_ge(ek_sb, b + 1)
                if b == 0:
                    pe.wait_ge(ve_sb, NT)
                    pe.wait_ge(ve_ones, 1)
                if b >= 1:
                    pe.wait_ge(ho_sb, b)
                for hh in range(H // HPC):
                    mm = pe.matmul(PS[:, 7, hh * HPC * V1:(hh + 1) * HPC * V1],
                                   EK[:, b % 2, hh * HPC:(hh + 1) * HPC, :],
                                   VE[:, NC * b, hh * HPC:(hh + 1) * HPC, :].rearrange("p h v -> p (h v)"),
                                   start=True, stop=True)
                mm.then_inc(kv_ps, 1)

            def apply(b):
                pe.wait_ge(kv_sb, b + 1)
                for hh in range(H // HPC):
                    mm = pe.matmul(PS[:, 7, hh * HPC * V1:(hh + 1) * HPC * V1], QKT[:, NC * b + 1, hh, :],
                                   KVS[:, hh, :], start=True, stop=True)
                mm.then_inc(ho_ps, 1)

            def pv(b, c):
                pe.wait_ge(c_sb, NC * b + c + 1)
                if c == 1:
                    pe.wait_ge(h0_sb, b + 1)
                elif b >= 1:
                    pe.wait_ge(h1_sb, b)
                for h in range(H):
                    mm = pe.matmul(PS[:, 6, h * V1:(h + 1) * V1], DEC[b % 2][:, c, h, :], VE[:, NC * b + c, h, :],
                                   start=True, stop=True)
                mm.then_inc(hd_ps, 1)

            scores(0, 0)
            pe.wait_ge(tok_rows, 3)
            for i in range(4):
                tr = pe.transpose(PS[:, 5, i * BH:(i + 1) * BH], ROWS[:, i, :], ident[0:BH, 0:BH])
            tr.then_inc(rowsT_ps, 1)
            args(0, 0, 4)
            scores(0, 1)
            state(0)
            for b in range(NB):
                more = b + 1 < NB
                if more:
                    args(b + 1, 0, 2)
                pv(b, 0)
                if more:
                    scores(b + 1, 0)
                apply(b)
                if more:
                    args(b + 1, 2, 4)
                pv(b, 1)
                if more:
                    scores(b + 1, 1)
                    state(b + 1)

            def p_xnT(b):
                pe.wait_ge(xn_sb, b + 1)
                if b >= 1:
                    pe.wait_ge(xnT_sb, b)
                if b == 0:
                    pe.wait_ge(c_sb, NT)
                    pe.wait_ge(dec_sb, 4 * NB)
                    pe.wait_ge(mu_step, 2)
                for k in range(DC):
                    for c in range(NC):
                        tr = pe.transpose(PS[:, 0, k * SEQ + c * P:k * SEQ + (c + 1) * P],
                                          XN[:, b % 6, c, k * P:(k + 1) * P], ident[:])
                tr.then_inc(xnT_ps, 1)

            def p_l(b):
                pe.wait_ge(xnT_sb, b + 1)
                if b >= 1:
                    pe.wait_ge(l_sb, NC * b)
                for c in range(NC):
                    for k in range(DC):
                        mm = pe.matmul(PS[:, 1, c * ES:(c + 1) * ES], XNT[:, b % 2, k, c * P:(c + 1) * P], MU[:, k],
                                       start=(k == 0), stop=(k == DC - 1))
                mm.then_inc(l_ps, 1)

            def p_lT(b):
                pe.wait_ge(l_sb, NC * (b + 1))
                if b >= 1:
                    pe.wait_ge(edt_sb, EC * b)
                for k in range(EC):
                    for c in range(NC):
                        tr = pe.transpose(PS[:, 2, k * SEQ + c * P:k * SEQ + (c + 1) * P],
                                          LSB[:, b % 2, c, k * P:(k + 1) * P], ident[:])
                tr.then_inc(lT_ps, 1)

            def p_ecT(b):
                pe.wait_ge(ec_sb, NC * (b + 1))
                if b >= 1:
                    pe.wait_ge(ecT_sb, b)
                for k in range(EC):
                    for c in range(NC):
                        tr = pe.transpose(PS[:, 4, k * SEQ + c * P:k * SEQ + (c + 1) * P],
                                          ECB[:, b % 2, c, k * P:(k + 1) * P], ident[:])
                tr.then_inc(ecT_ps, 1)

            def p_edT(b):
                pe.wait_ge(edt_n, EC * (b + 1))
                if b >= 1:
                    pe.wait_ge(ed_sb, b)
                for c in range(NC):
                    for k in range(EC):
                        tr = pe.transpose(PS[:, 3, c * ES + k * P:c * ES + (k + 1) * P],
                                          EDT[:, b % 2, k, c * P:(c + 1) * P], ident[:])
                tr.then_inc(edT_ps, 1)

            def p_slot(b):
                pe.wait_ge(ed_sb, b + 1)
                if b >= 1:
                    pe.wait_ge(slot_sb, DC * b)
                for k in range(DC):
                    for c in range(NC):
                        mm = pe.matmul(PS[:, 5, k * ES:(k + 1) * ES], XN[:, b % 6, c, k * P:(k + 1) * P], ED[:, b % 2, c],
                                       start=(c == 0), stop=(c == NC - 1))
                mm.then_inc(slot_ps, 1)

            for k in range(NB + 5):
                if 4 <= k <= NB + 3:
                    p_edT(k - 4)
                if 3 <= k <= NB + 2:
                    p_ecT(k - 3)
                if k < NB:
                    p_xnT(k)
                if 1 <= k <= NB:
                    p_l(k - 1)
                if 2 <= k <= NB + 1:
                    p_lT(k - 2)
                if 4 <= k <= NB + 3:
                    p_slot(k - 4)

            pe.wait_ge(slot_sb, DC * NB)
            pe.wait_ge(moe_in, 16 * (DC + 2 + EC * EPC))
            for e in range(E):
                q, p = e % 2, e // 2
                for k in range(DC):
                    mm = pe.matmul(PS[q * HID:(q + 1) * HID, p // 4, (p % 4) * P:(p % 4 + 1) * P], W1[:, k, e, :],
                                   SIN[k][:, e].rearrange("p b s -> p (b s)"), start=(k == 0), stop=(k == DC - 1))
                if e % 8 == 7:
                    mm.then_inc(hid_ps, 1)
            for k in range(DC):
                for p in range(EP):
                    if k == 0 and p % 4 == 0:
                        pe.wait_ge(hid_sb, 2 * (p // 4) + 2)
                    mm = pe.matmul(PS[:, (2 + 4 * k + p // 2) % 8, (p % 2) * 2 * P:(p % 2 + 1) * 2 * P],
                                   W2[:, p, k * P:(k + 1) * P], HSZ[:, p].rearrange("p q n -> p (q n)"),
                                   start=True, stop=True)
                    if p % 4 == 3:
                        mm.then_inc(so_ps, 1)
            pe.wait_ge(soa_sb, 4)
            pe.wait_ge(sov_sb, 4)

            def soT(b):
                if b >= 2:
                    pe.wait_ge(so_sb, b - 1)
                for k in range(EC):
                    for c in range(DC):
                        tr = pe.transpose(PS[:, 2 + b % 2, k * D + c * P:k * D + (c + 1) * P],
                                          SOT[:, c, b, k * EPC:(k + 1) * EPC, :].rearrange("p e s -> p (e s)"), ident[:])
                tr.then_inc(soT_ps, 1)

            def comb(b):
                pe.wait_ge(so_sb, b + 1)
                if b >= 2:
                    pe.wait_ge(y_sb, NC * (b - 1))
                for c in range(NC):
                    for k in range(EC):
                        mm = pe.matmul(PS[:, 4 + b % 2, c * D:(c + 1) * D], ECT[:, b, k, c * P:(c + 1) * P],
                                       SO[:, b % 2, k], start=(k == 0), stop=(k == EC - 1))
                mm.then_inc(y_ps, 1)

            soT(0)
            for b in range(NB):
                if b + 1 < NB:
                    soT(b + 1)
                comb(b)

        @block.vector
        def _(dve):
            def weights():
                dve.wait_ge(wT_ps, 1)
                dve.wait_ge(wz_zero, 1)
                dve.tensor_copy(WTA[:].rearrange("p k g -> p (k g)"), PS[:, 3, 0:96]).then_inc(wt_step, 1)
                dve.tensor_copy(B1[:], PS[:, 3, 96:96 + EP]).then_inc(b1_sb, 1)
                dve.wait_ge(wt_step, 1)
                wz = WZ[:, :, BH - H:BH - H + 2 * BH].rearrange("p k (g r) -> p k g r", g=2)[:, :, :, 0:H]
                wta = WTA[:].rearrange("p k (g h) -> p k g h", g=2)
                dve.tensor_copy(wz[:, 0:2], wta[:, 0:2]).then_inc(wt_step, 1)
                dve.tensor_tensor(wz[:, 2:4], wta[:, 2:4], wta[:, 4:6], ALU.add).then_inc(wt_step, 1)

            def head_means(b):
                dve.wait_ge(c_in[b], 16 * NC)
                for c in range(NC):
                    dve.tensor_reduce(VM[:, NC * b + c], CX[c][:, b].rearrange("p (h v) -> p h v", h=H), AX.X,
                                      ALU.add).then_inc(v_sum, 1)
                dve.wait_ge(v_sum, NC * (b + 1))
                dve.tensor_scalar(VM[:, NC * b:NC * b + NC], VM[:, NC * b:NC * b + NC], 1.0 / HD, None,
                                  ALU.mult).then_inc(v_mean, 1)

            def stats(b):
                dve.wait_ge(x_in[b], 16)
                for t in (NC * b, NC * b + 1):
                    dve.bn_stats(ST[:, t], X[:, t]).then_inc(ln_st, 1)
                for t in (NC * b, NC * b + 1):
                    dve.wait_ge(ln_st, t + 1)
                    dve.bn_aggr(MV[:, t], ST[:, t]).then_inc(ln_mv, 1)

            def norm(b):
                dve.wait_ge(ln_rs, b + 1)
                for t in (NC * b, NC * b + 1):
                    dve.tensor_scalar(Q[:, t], X[:, t], MV[:, t, 0:1], RS[:, t:t + 1],
                                      ALU.subtract, ALU.mult).then_inc(q_sb, 1)
            dve.memset(WZ[:], 0.0).then_inc(wz_zero, 1)
            stats(0)
            stats(1)
            for b in range(NB):
                norm(b)
                if b == 0:
                    weights()
                if b + 2 < NB:
                    stats(b + 2)
                head_means(b)
                if b == 2:
                    dve.wait_ge(mu_sum, 1)
                    dve.tensor_scalar(MUN[:], PS[:, 3, 0:ES], NORM_FLOOR_SQ, None, ALU.max).then_inc(mu_max, 1)
            dve.wait_ge(mu_sqrt, 1)
            dve.reciprocal(MUN[:], MUN[:]).then_inc(mu_step, 1)
            dve.wait_ge(mu_step, 1)
            dve.tensor_tensor(MU[:], MU[:], MUN[:].unsqueeze(1).to_broadcast([P, DC, ES]), ALU.mult).then_inc(mu_step, 1)
            dve.wait_ge(gate_ps, NB)
            dve.wait_ge(vec_in, 16 * NVEC)
            dve.tensor_scalar(FS[:], PS[BH:2 * BH, 2, 0:SEQ], BG[BH:2 * BH, 0:1], None, ALU.add).then_inc(row_step, 1)
            dve.wait_ge(row_step, 1)
            dve.scalar_tensor_tensor(out=NA[:], in0=FS[:], scalar=-1.0, in1=FS[:], op0=ALU.mult,
                                     op1=ALU.min).then_inc(row_step, 1)
            dve.wait_ge(sig_l, 1)
            dve.scalar_tensor_tensor(out=LS[:], in0=FS[:], scalar=0.0, in1=LF[:], op0=ALU.min,
                                     op1=ALU.subtract).then_inc(row_step, 1)
            dve.wait_ge(row_step, 3)
            dve.tensor_tensor_scan(CS[:], ones[0:BH, 0:1].to_broadcast([BH, SEQ]), LS[:], 0.0,
                                   ALU.mult, ALU.add).then_inc(row_step, 1)
            dve.wait_ge(row_step, 4)
            dve.scalar_tensor_tensor(out=G[:], in0=PS[0:BH, 2, 0:SEQ], scalar=BG[0:BH, 0:1], in1=CS[:], op0=ALU.add,
                                     op1=ALU.subtract).then_inc(row_step, 1)
            dve.wait_ge(row_step, 5)
            dve.tensor_tensor_scan(M[:], G[:], G[:], NEG_BIG, ALU.max, ALU.max).then_inc(row_step, 1)
            dve.wait_ge(row_step, 6)
            dve.tensor_scalar(NM[:], M[:], -1.0, None, ALU.mult).then_inc(row_step, 1)
            dve.tensor_tensor(CM[:], CS[:], M[:], ALU.add).then_inc(row_step, 1)
            dve.wait_ge(row_step, 8)
            dve.tensor_copy(MHL[:, 0], NM[:]).then_inc(split, 1)
            dve.tensor_copy(GHL[:, 0], G[:]).then_inc(split, 1)
            dve.wait_ge(split, 2)
            dve.tensor_tensor(MHL[:, 1], NM[:], MHL[:, 0].bitcast(F32), ALU.subtract).then_inc(split, 1)
            dve.tensor_tensor(GHL[:, 1], G[:], GHL[:, 0].bitcast(F32), ALU.subtract).then_inc(split, 1)
            dve.wait_ge(rowsT_ps, 1)
            dve.tensor_copy(TT[:].rearrange("p r n -> p (r n)"), PS[:, 5, 0:4 * BH]).then_inc(rowsT_sb, 1)
            def kv(b):
                dve.wait_ge(kv_ps, b + 1)
                if b == 0:
                    dve.wait_ge(const_step, 4)
                if b >= 1:
                    dve.wait_ge(ho_ps, b)
                dve.tensor_tensor(KVS[:], PS[:, 7, 0:H * V1].rearrange("p (k v) -> p k v", k=2),
                                  blockmask[:].unsqueeze(1).to_broadcast([P, 2, HPC * V1]), ALU.mult).then_inc(kv_sb, 1)

            def cmul(b):
                for c in range(NC):
                    dve.wait_ge(s_ps, NC * b + c + 1)
                    dve.wait_ge(dec_mask, NC * b + c + 1)
                    d = DEC[b % 2][:, c].rearrange("p h i -> p (h i)")
                    dve.tensor_tensor(d, PS[:, 2 * c:2 * c + 2, :].rearrange("p k n -> p (k n)"),
                                      d, ALU.mult).then_inc(c_sb, 1)

            def h1(b):
                u = b % 2
                f = TT[:, 3, H * b:H * b + H].unsqueeze(2).to_broadcast([P, H, V1])
                dve.wait_ge(ho_ps, b + 1)
                if b >= 1:
                    dve.wait_ge(h1_sb, b)
                dve.tensor_tensor(HT1[:], PS[:, 7, 0:H * V1].rearrange("p (h v) -> p h v", h=H), f,
                                  ALU.mult).then_inc(ho_sb, 1)
                dve.wait_ge(hd_ps, 2 * b + 2)
                dve.wait_ge(ho_sb, b + 1)
                dve.tensor_tensor(HB[:, u, 1], PS[:, 6, 0:H * V1].rearrange("p (h v) -> p h v", h=H), HT1[:],
                                  ALU.add).then_inc(h1_sb, 1)

            def sm(b, i):
                return SM[:, b % 2, i].rearrange("p (c h) -> p c h", c=NC)

            def post_a(b):
                u, st, n = b % 2, post_step, 8 * b
                rs = HB[:, u, :, :, HD]
                dve.wait_ge(h1_sb, b + 1)
                dve.wait_ge(h0_sb, b + 1)
                dve.scalar_tensor_tensor(out=sm(b, 1), in0=rs, scalar=-1.0, in1=rs, op0=ALU.mult,
                                         op1=ALU.max).then_inc(st, 1)
                dve.wait_ge(st, n + 1)
                dve.scalar_tensor_tensor(out=sm(b, 2), in0=TT[:, 0:2, H * b:H * b + H], scalar=TAU, in1=sm(b, 1),
                                         op0=ALU.mult, op1=ALU.max).then_inc(st, 1)
                dve.wait_ge(st, n + 2)
                dve.tensor_scalar(SM[:, u, 2], SM[:, u, 2], TAU * 1e-6, None, ALU.add).then_inc(st, 1)
                dve.wait_ge(st, n + 3)
                dve.reciprocal(SM[:, u, 3], SM[:, u, 2]).then_inc(st, 1)
                dve.wait_ge(st, n + 4)
                dve.tensor_tensor(SM[:, u, 4], SM[:, u, 3], SM[:, u, 3], ALU.mult).then_inc(st, 1)
                dve.wait_ge(sq_sb, b + 1)
                dve.tensor_reduce(sm(b, 5), SQ[:], AX.X, ALU.add).then_inc(st, 1)
                dve.wait_ge(st, n + 6)
                dve.scalar_tensor_tensor(out=SM[:, u, 6], in0=SM[:, u, 5], scalar=1.0 / HD, in1=SM[:, u, 4],
                                         op0=ALU.mult, op1=ALU.mult).then_inc(st, 1)

            def post_b(b):
                u, st, n = b % 2, post_step, 8 * b
                dve.wait_ge(gn_rs, b + 1)
                dve.tensor_tensor(SM[:, u, 9], SM[:, u, 8], SM[:, u, 3], ALU.mult).then_inc(st, 1)
                dve.wait_ge(st, n + 8)
                fac = sm(b, 9).unsqueeze(3).to_broadcast([P, NC, H, HD]).rearrange("p c h v -> p (c h) v")
                dve.tensor_tensor(NRM[:, u].rearrange("p c (h v) -> p (c h) v", h=H),
                                  HB[:, u, :, :, 0:HD].rearrange("p c h v -> p (c h) v"), fac, ALU.mult).then_inc(nrm_sb, 1)
                dve.wait_ge(nrm_sb, b + 1)
                dve.tensor_tensor(NRM[:, u], NRM[:, u], GNW[:].unsqueeze(1).to_broadcast([P, NC, D]),
                                  ALU.mult).then_inc(gw_sb, 1)
                dve.wait_ge(gw_sb, b + 1)
                dve.wait_ge(xb_sb, b + 1)
                if b == 0:
                    dve.wait_ge(qk_ps, NT)
                dve.tensor_tensor(Q[:, NC * b:NC * b + NC, :], NRM[:, u], X[:, NC * b:NC * b + NC, :],
                                  ALU.add).then_inc(x1_sb, 1)

            kv(0)
            cmul(0)
            for b in range(NB):
                h1(b)
                if b + 1 < NB:
                    kv(b + 1)
                    cmul(b + 1)
                if b >= 1:
                    post_b(b - 1)
                post_a(b)
            post_b(NB - 1)

            def lstats(b):
                dve.wait_ge(x1_sb, b + 1)
                for t in (NC * b, NC * b + 1):
                    dve.bn_stats(ST[:, t], Q[:, t]).then_inc(l_st, 1)
                for t in (NC * b, NC * b + 1):
                    dve.wait_ge(l_st, t + 1)
                    dve.bn_aggr(MV[:, t], ST[:, t]).then_inc(l_mv, 1)
                dve.wait_ge(l_mv, NC * (b + 1))
                dve.tensor_scalar(SS[:, b, 4], MV[:, NC * b:NC * b + NC, 1], 1.0 + LN_EPS, LN_EPS * LN_EPS,
                                  ALU.mult, ALU.add).then_inc(l_var, 1)

            def lnorm(b):
                dve.wait_ge(l_rs, b + 1)
                if b >= 2:
                    dve.wait_ge(xg_sb, b - 1)
                for c in range(NC):
                    t = NC * b + c
                    dve.tensor_scalar(XH[:, b % 2, c], Q[:, t], MV[:, t, 0:1], SS[:, b, 6, c:c + 1],
                                      ALU.subtract, ALU.mult).then_inc(xh_sb, 1)

            def rowmax(b):
                dve.wait_ge(l_sb, NC * (b + 1))
                dve.tensor_reduce(SS[:, b, 7], LSB[:, b % 2], AX.X, ALU.max, negate=True).then_inc(rowmax_sb, 1)

            def colmax(b):
                dve.wait_ge(lT_ps, b + 1)
                dve.tensor_reduce(DM[:, b], PS[:, 2, :].rearrange("p (k n) -> p k n", k=EC), AX.X, ALU.max,
                                  negate=True).then_inc(colmax_sb, 1)

            def dnorm(b):
                dve.wait_ge(edt_sb, EC * (b + 1))
                dve.reciprocal(DR[:, b], DS[:, b]).then_inc(edt_step, 1)
                dve.wait_ge(edt_step, b + 1)
                for k in range(EC):
                    dve.tensor_scalar(EDT[:, b % 2, k], EDT[:, b % 2, k], DR[:, b, k:k + 1], None,
                                      ALU.mult).then_inc(edt_n, 1)

            def ecT(b):
                dve.wait_ge(ecT_ps, b + 1)
                dve.tensor_copy(ECT[:, b].rearrange("p k n -> p (k n)"), PS[:, 4, :]).then_inc(ecT_sb, 1)

            def edc(b):
                dve.wait_ge(edT_ps, b + 1)
                if b >= 2:
                    dve.wait_ge(slot_ps, b - 1)
                dve.tensor_copy(ED[:, b % 2].rearrange("p c e -> p (c e)"), PS[:, 3, :]).then_inc(ed_sb, 1)

            lstats(0)
            lnorm(0)
            lstats(1)
            for k in range(NB + 5):
                if 3 <= k <= NB + 2:
                    dnorm(k - 3)
                if 4 <= k <= NB + 3:
                    edc(k - 4)
                if 3 <= k <= NB + 2:
                    ecT(k - 3)
                if k + 1 < NB:
                    lnorm(k + 1)
                if k + 2 < NB:
                    lstats(k + 2)
                if 2 <= k <= NB + 1:
                    colmax(k - 2)
                if 1 <= k <= NB:
                    rowmax(k - 1)
            dve.wait_ge(ec_sb, NT)
            dve.reciprocal(RCI[:], RC[:]).then_inc(rc_sb, 1)

            for h in range(2):
                dve.wait_ge(hid_ps, h + 1)
                dve.tensor_tensor(HPB[:, 4 * h:4 * h + 4, :], PS[:, h, :].rearrange("p (e n) -> p e n", e=4),
                                  B1[:, 4 * h:4 * h + 4].unsqueeze(2).to_broadcast([P, 4, P]), ALU.add).then_inc(hpb_sb, 1)
            for k in range(DC):
                dve.wait_ge(so_ps, 2 * k + 2)
                for g in range(2, 4):
                    dve.tensor_copy(SOT[:, k, :, 4 * g:4 * g + 4, :].rearrange("p b e s -> p e b s"),
                                    PS[:, (2 + 4 * k + g) % 8, :].rearrange("p (e b s) -> p e b s", e=4, b=NB)).then_inc(sov_sb, 1)

            def so(b):
                dve.wait_ge(soT_ps, b + 1)
                if b >= 2:
                    dve.wait_ge(y_ps, b - 1)
                if b == 0:
                    dve.wait_ge(moe_in, 16 * (DC + 2 + EC * EPC))
                dve.tensor_tensor(SO[:, b % 2], PS[:, 2 + b % 2, :].rearrange("p (k d) -> p k d", k=EC), B2R[:],
                                  ALU.add).then_inc(so_sb, 1)

            def yy(b):
                dve.wait_ge(y_ps, b + 1)
                if b >= 2:
                    dve.wait_ge(y_out[b % 2], 16 * (b // 2))
                if b == 0:
                    dve.wait_ge(rc_sb, 1)
                for c in range(NC):
                    dve.scalar_tensor_tensor(out=Y[:, b % 2, c], in0=PS[:, 4 + b % 2, c * D:(c + 1) * D],
                                             scalar=RCI[:, b, c:c + 1], in1=Q[:, NC * b + c], op0=ALU.mult,
                                             op1=ALU.add).then_inc(y_sb, 1)
            so(0)
            for b in range(NB):
                if b + 1 < NB:
                    so(b + 1)
                yy(b)


_INS = ['x', 'ctx_1024', 'L0_xattn_Wi_w', 'L0_xattn_Wi_b', 'L0_xattn_Wf_w', 'L0_xattn_Wf_b', 'L0_xattn_gn_w',
        'L0_xattn_gn_b', 'L0_ffn_ln_gamma', 'L0_ffn_ln_beta', 'L0_ffn_mu', 'L0_ffn_scale', 'L0_ffn_w1',
        'L0_ffn_b1', 'L0_ffn_w2', 'L0_ffn_b2']


def kernel(**inputs):
    import concourse.bacc as _bacc
    from concourse.bass_utils import run_bass_kernel_spmd as _run

    nc = _bacc.Bacc("TRN2", target_bir_lowering=False, num_devices=1)
    arrays, args = {}, []
    for name in _INS:
        a = np.ascontiguousarray(inputs[name])
        arrays[f"in_{name}"] = a
        args.append(nc.dram_tensor(f"in_{name}", a.shape, mybir.dt.from_np(a.dtype), kind="ExternalInput").ap())
    y = nc.dram_tensor("out_0", tuple(inputs['x'].shape), F32, kind="ExternalOutput").ap()
    xattn_ffn(nc, *args, y)
    r = _run(nc, [arrays], core_ids=[0])
    return r.results[0]["out_0"]
```

```python
from contextlib import ExitStack

import numpy as np

import concourse.bass as bass
from concourse import mybir

F32 = mybir.dt.float32
F32R = mybir.dt.float32r
ALU = mybir.AluOpType
ACT = mybir.ActivationFunctionType
AX = mybir.AxisListType

P = 128
TAU = 32.0 ** 0.5
LN_EPS = 1e-5
NORM_FLOOR_SQ = 1e-24
NEG_BIG = -3.0e38


def xattn_ffn(nc, x, ctx_in, Wi_w, Wi_b, Wf_w, Wf_b, gn_w, gn_b,
              ln_gamma, ln_beta, mu, scale, w1, b1, w2, b2, out):
    NB, SEQ, D = x.shape
    H = Wi_w.shape[0]
    HD = D // H
    V1 = HD + 1
    NC = SEQ // P
    NT = NB * NC
    _, E, S = mu.shape
    HID = w1.shape[2]
    ES = E * S
    DC = D // P
    EC = ES // P
    EP = E // 2
    BH = NB * H
    GB = NB // 2
    GH = GB * H
    HPC = P // HD
    EPC = P // S
    RB = 32
    assert NC == 2 and DC == 2 and EC == 2 and H == 8 and HID == 64 and NB * S == P

    with ExitStack() as stack:
        def sb(name, shape, dt=F32):
            return stack.enter_context(nc.sbuf_tensor(name, shape, dt))

        def sem(name):
            return stack.enter_context(nc.semaphore(name))

        X = sb("X", [P, NT, D])
        CX = [sb("C0", [P, NB, D]), sb("C1", [P, NB, D])]
        D0 = sb("D0", [P, NC * H * P])
        DEC = [D0[:].rearrange("p (c h i) -> p c h i", c=NC, h=H),
               CX[1][:].rearrange("p b d -> p (b d)").rearrange("p (c h i) -> p c h i", c=NC, h=H)]
        SIN = [v.rearrange("p c h i -> p (c h i)").rearrange("p (e b s) -> p e b s", e=E, b=NB) for v in DEC]
        VE = sb("VE", [P, NT, H, V1])
        ECT = VE[:].rearrange("p t h v -> p (t h v)")[:, 0:NB * EC * SEQ].rearrange(
            "p (b k n) -> p b k n", b=NB, k=EC)
        Q = sb("Q", [P, NT, D])
        QKT = sb("QKT", [P, NT, 2 * DC, P])
        flat = QKT[:].rearrange("p t k n -> p (t k n)")
        W = NC * D
        XN = flat[:, 0:6 * W].rearrange("p (u c d) -> p u c d", u=6, c=NC)
        XNT = flat[:, 6 * W:8 * W].rearrange("p (u k n) -> p u k n", u=2, k=DC)
        LSB = flat[:, 8 * W:10 * W].rearrange("p (u c e) -> p u c e", u=2, c=NC)
        ECB = flat[:, 10 * W:12 * W].rearrange("p (u c e) -> p u c e", u=2, c=NC)
        EDT = flat[:, 12 * W:14 * W].rearrange("p (u k n) -> p u k n", u=2, k=EC)
        ED = flat[:, 14 * W:16 * W].rearrange("p (u c e) -> p u c e", u=2, c=NC)
        SOT = flat[:, 0:8 * W].rearrange("p (k b e s) -> p k b e s", k=DC, b=NB, e=E)
        SO = flat[:, 8 * W:10 * W].rearrange("p (u k d) -> p u k d", u=2, k=EC)
        Y = flat[:, 10 * W:12 * W].rearrange("p (u c d) -> p u c d", u=2, c=NC)
        HPB = flat[:, 12 * W:14 * W].rearrange("p (e n) -> p e n", e=EP)
        QZ = sb("QZ", [P, 2, HPC, NC, DC, P])
        HSZ = QZ[:, 0].rearrange("p r c k i -> p (r c k i)").rearrange("p (e q n) -> p e q n", e=EP, q=2)
        XNQ = QZ[:, 1].rearrange("p r c k i -> p (r c k i)").rearrange("p (u c d) -> p u c d", u=4, c=NC)
        B2R = XNQ[:, 2]
        MROW = sb("MROW", [RB + 4, H, SEQ], F32R)
        GROW = sb("GROW", [RB + 4, H, SEQ], F32R)
        MHL = sb("MHL", [GH, 2, 2, SEQ], F32R)
        GHL = sb("GHL", [GH, 2, 2, SEQ], F32R)
        ident = sb("ident", [P, P])
        identr = sb("identr", [P, P], F32R)
        late = sb("late", [P, P], F32R)
        ones = sb("ones", [P, P])
        blockmask = sb("blockmask", [P, HPC * V1])
        neghalf = sb("neghalf", [P, NC * H])
        GNW = sb("GNW", [P, D])
        GNB = sb("GNB", [P, D])
        GAM = sb("GAM", [P, D])
        BET = sb("BET", [P, D])
        SCL = sb("SCL", [P, 1])
        BG = sb("BG", [2 * GH, 1])
        WW = sb("WW", [2 * H, 3 * D])
        WTA = sb("WTA", [P, 6, 2 * H])
        WZ = sb("WZ", [P, 4, 2 * GH + GH - H])
        B1L = sb("B1L", [EP, P])
        B1 = sb("B1", [P, EP])
        W1 = sb("W1", [P, DC, E, HID])
        W2 = sb("W2", [P, EP, D])
        MU = sb("MU", [P, DC, ES])
        MUN = sb("MUN", [P, ES])
        ST = sb("ST", [P, NT, 6])
        MV = sb("MV", [P, NT, 2])
        LV = sb("LV", [P, NT])
        RS = sb("RS", [P, NT])
        VM = sb("VM", [P, NT, H])
        JNK = sb("JNK", [P, D])
        GT = sb("GT", [2 * GH, SEQ])
        FA = JNK[0:2 * GH]
        LS = sb("LS", [GH, SEQ])
        CS = sb("CS", [GH, SEQ])
        G = sb("G", [GH, 2, SEQ])
        M = sb("M", [GH, 2, SEQ])
        NM = sb("NM", [GH, 2, SEQ])
        CM = sb("CM", [GH, SEQ])
        ROWS = sb("ROWS", [GH, 4, P])
        TT = sb("TT", [P, 4, BH])
        EK = sb("EK", [P, 2, H, HD])
        KVS = sb("KVS", [P, 2, HPC * V1])
        HT1 = sb("HT1", [P, H, V1])
        HB = sb("HB", [P, 2, NC, H, V1])
        SQ = sb("SQ", [P, NC, H, HD])
        SM = sb("SM", [P, 2, 10, NC * H])
        NRM = sb("NRM", [P, 2, NC, D])
        MUQ = NRM[:, 0]
        SS = sb("SS", [P, NB, 8, NC])
        RC = sb("RC", [P, NB, NC])
        RCI = sb("RCI", [P, NB, NC])
        DM = sb("DM", [P, NB, EC])
        DS = sb("DS", [P, NB, EC])
        DR = sb("DR", [P, NB, EC])
        PS = stack.enter_context(nc.psum_tensor("PS", [P, 8, 512], F32))

        x_in = [sem(f"x_in{b}") for b in range(NB)]
        c_in = [sem(f"c_in{b}") for b in range(NB)]
        w_in = sem("w_in")
        mu_in = sem("mu_in")
        vec_in = sem("vec_in")
        bias_in = sem("bias_in")
        moe_in = sem("moe_in")

        rows_in = [sem("rows_in0"), sem("rows_in1")]
        qz_in = [sem("qz_in0"), sem("qz_in1")]
        y_out = [sem("y_out0"), sem("y_out1")]
        consts = sem("consts")
        const_step = sem("const_step")
        late_step = sem("late_step")
        wT_ps = sem("wT_ps")
        wt_step = sem("wt_step")
        b1_sb = sem("b1_sb")
        musq = sem("musq")
        mu_sum = sem("mu_sum")
        mu_max = sem("mu_max")
        mu_sqrt = sem("mu_sqrt")
        mu_step = sem("mu_step")
        ln_st = sem("ln_st")
        ln_mv = sem("ln_mv")
        ln_var = sem("ln_var")
        ln_rs = sem("ln_rs")
        q_sb = sem("q_sb")
        qk_ps = sem("qk_ps")
        qk_sb = sem("qk_sb")
        ve_ones = sem("ve_ones")
        v_sum = sem("v_sum")
        v_mean = sem("v_mean")
        rows_one = sem("rows_one")
        qz_zero = sem("qz_zero")
        wz_zero = sem("wz_zero")
        hs_zero = sem("hs_zero")
        hpb_sb = sem("hpb_sb")
        ve_sb = sem("ve_sb")
        gate_ps = sem("gate_ps")
        row_step = sem("row_step")
        sig_e = sem("sig_e")
        sig_l = sem("sig_l")
        tok_rows = sem("tok_rows")
        split = sem("split")
        rowsT_ps = sem("rowsT_ps")
        rowsT_sb = sem("rowsT_sb")
        arg_ps = sem("arg_ps")
        dec_sb = sem("dec_sb")
        s_ps = sem("s_ps")
        c_sb = sem("c_sb")
        ek_sb = sem("ek_sb")
        kv_ps = sem("kv_ps")
        kv_sb = sem("kv_sb")
        ho_ps = sem("ho_ps")
        ho_sb = sem("ho_sb")
        hd_ps = sem("hd_ps")
        h0_sb = sem("h0_sb")
        h1_sb = sem("h1_sb")
        post_step = sem("post_step")
        sq_sb = sem("sq_sb")
        gn_var = sem("gn_var")
        gn_rs = sem("gn_rs")
        nrm_sb = sem("nrm_sb")
        xb_sb = sem("xb_sb")
        gw_sb = sem("gw_sb")
        x1_sb = sem("x1_sb")
        l_st = sem("l_st")
        l_mv = sem("l_mv")
        l_var = sem("l_var")
        l_rs = sem("l_rs")
        xh_sb = sem("xh_sb")
        xg_sb = sem("xg_sb")
        xn_sb = sem("xn_sb")
        ss_sb = sem("ss_sb")
        rn_step = sem("rn_step")
        rn_sb = sem("rn_sb")
        xnT_ps = sem("xnT_ps")
        xnT_sb = sem("xnT_sb")
        l_ps = sem("l_ps")
        l_sb = sem("l_sb")
        rowmax_sb = sem("rowmax_sb")
        ec_sb = sem("ec_sb")
        lT_ps = sem("lT_ps")
        colmax_sb = sem("colmax_sb")
        edt_sb = sem("edt_sb")
        edt_step = sem("edt_step")
        edt_n = sem("edt_n")
        edT_ps = sem("edT_ps")
        ed_sb = sem("ed_sb")
        ecT_ps = sem("ecT_ps")
        ecT_sb = sem("ecT_sb")
        rc_sb = sem("rc_sb")
        slot_ps = sem("slot_ps")
        slot_sb = sem("slot_sb")
        hid_ps = sem("hid_ps")
        hid_sb = sem("hid_sb")
        so_ps = sem("so_ps")
        soa_sb = sem("soa_sb")
        sov_sb = sem("sov_sb")
        soT_ps = sem("soT_ps")
        so_sb = sem("so_sb")
        y_ps = sem("y_ps")
        y_sb = sem("y_sb")

        def xnb(b):
            return XN[:, b] if b < 6 else XNQ[:, b - 6]

        block = stack.enter_context(nc.Block())

        NVEC = 5

        @block.sync
        def _(sp):
            def bc(v, n=P):
                return v.partition_broadcast(n)

            def tok(a, b):
                return a[b].rearrange("(c p) d -> p c d", p=P)
            def load(b):
                sp.dma_start(X[:, NC * b:NC * b + NC, :], tok(x, b)).then_inc(x_in[b], 16)
                for c in range(NC):
                    sp.dma_start(CX[c][:, b, :], ctx_in[b, c * P:(c + 1) * P, :]).then_inc(c_in[b], 16)
            load(0)
            sp.dma_start(WW[0:H, :], Wi_w).then_inc(w_in, 16)
            sp.dma_start(WW[H:2 * H, :], Wf_w).then_inc(w_in, 16)
            sp.dma_start(B1L[:], b1.rearrange("(p q) h -> p (q h)", q=2)).then_inc(w_in, 16)
            load(1)
            sp.dma_start(MU[:], mu.rearrange("(k p) e s -> p k (e s)", p=P)).then_inc(mu_in, 16)
            for b in range(2, NB):
                load(b)

            for g, v in ((0, Wi_b), (1, Wf_b)):
                for b in range(GB):
                    sp.dma_start(BG[g * GH + H * b:g * GH + H * b + H, 0:1], v.unsqueeze(1)).then_inc(bias_in, 16)

            def head_copies(b):
                for i in range(HPC):
                    rows = slice(HD * i, HD * i + HD)
                    sp.dma_start(QZ[rows, b % 2, i], QKT[rows, NC * b:NC * b + NC, 0:DC, :]).then_inc(qz_in[b % 2], 16)
            sp.wait_ge(qz_zero, 2)
            for b in range(2):
                sp.wait_ge(qk_sb, NC * (b + 1))
                head_copies(b)
            sp.dma_start(GNW[:], bc(gn_w)).then_inc(vec_in, 16)
            sp.dma_start(GNB[:], bc(gn_b)).then_inc(vec_in, 16)
            sp.dma_start(GAM[:], bc(ln_gamma)).then_inc(vec_in, 16)
            sp.dma_start(BET[:], bc(ln_beta)).then_inc(vec_in, 16)
            sp.dma_start(SCL[:], bc(scale)).then_inc(vec_in, 16)
            for k in range(DC):
                sp.dma_start(W1[:, k], w1[:, k * P:(k + 1) * P, :].rearrange("e p h -> p e h")).then_inc(moe_in, 16)
            for q in range(2):
                sp.dma_start(W2[q * HID:(q + 1) * HID], w2.rearrange("(p q) h d -> q h p d", q=2)[q]).then_inc(moe_in, 16)
            sp.wait_ge(rows_one, 2)
            for b in range(NB):
                if b % GB == 0:
                    sp.wait_ge(split, 4 * (b // GB + 1))
                hb = slice(H * (b % GB), H * (b % GB) + H)
                if b >= 2:
                    sp.wait_ge(arg_ps, 4 * (b - 1))
                r0 = RB * (b % 2)
                for a in range(2):
                    sp.dma_start(MROW[r0 + a:r0 + a + 1].bitcast(F32), MHL[hb, b // GB, a, :].bitcast(F32)).then_inc(rows_in[b % 2], 16)
                    sp.dma_start(GROW[r0 + 2 + a:r0 + 3 + a].bitcast(F32), GHL[hb, b // GB, a, :].bitcast(F32)).then_inc(rows_in[b % 2], 16)
                if 1 <= b < NB - 1:
                    sp.wait_ge(s_ps, DC * NC * b)
                    head_copies(b + 1)
            sp.wait_ge(s_ps, DC * NC * NB)
            for k in range(EC):
                for e in range(EPC):
                    sp.dma_start(B2R[e * S:(e + 1) * S, k, :], bc(b2[k * EPC + e], S)).then_inc(moe_in, 16)
            for b in range(NB):
                sp.wait_ge(y_sb, NC * (b + 1))
                sp.dma_start(out[b].rearrange("(c p) d -> p c d", p=P), Y[:, b % 2]).then_inc(y_out[b % 2], 16)
            sp.wait_ge(y_out[0], 16 * (NB // 2))
            sp.wait_ge(y_out[1], 16 * (NB // 2))

        @block.gpsimd
        def _(pool):
            def centre(b):
                pool.wait_ge(v_mean, b + 1)
                for c in range(NC):
                    pool.tensor_tensor(VE[:, NC * b + c, :, 0:HD], CX[c][:, b].rearrange("p (h v) -> p h v", h=H),
                                       VM[:, NC * b + c].unsqueeze(2).to_broadcast([P, H, HD]),
                                       ALU.subtract).then_inc(ve_sb, 1)

            def masks():
                late_f = HT1[:].rearrange("p h v -> p (h v)")[:, 0:P]
                bm = blockmask[:].rearrange("p (r v) -> p r v", r=HPC)
                pool.affine_select(out=bm, in_=bm, compare_op=ALU.is_ge, fill=0.0, base=0,
                                   pattern=[[-HD, HPC], [0, V1]], channel_multiplier=1).then_inc(const_step, 1)
                pool.wait_ge(const_step, 3)
                pool.affine_select(out=bm, in_=bm, compare_op=ALU.is_gt, fill=0.0, base=HD,
                                   pattern=[[HD, HPC], [0, V1]], channel_multiplier=-1).then_inc(const_step, 1)
                pool.memset(late_f, 0.0).then_inc(late_step, 1)
                pool.tensor_copy(identr[:], ident[:]).then_inc(late_step, 1)
                pool.wait_ge(late_step, 2)
                pool.affine_select(out=late_f, in_=late_f, compare_op=ALU.is_ge, fill=-1e30, base=0,
                                   pattern=[[1, P]], channel_multiplier=-1).then_inc(late_step, 1)
                pool.wait_ge(late_step, 3)
                pool.tensor_copy(late[:], late_f).then_inc(late_step, 1)

            def residual(b):
                xb = X[:, NC * b:NC * b + NC, :]
                pool.tensor_tensor(xb, xb, GNB[:].unsqueeze(1).to_broadcast([P, NC, D]), ALU.add).then_inc(xb_sb, 1)

            pool.memset(ident[:], 1.0).then_inc(const_step, 1)
            pool.memset(ones[:], 1.0).then_inc(consts, 1)
            pool.memset(blockmask[:], 1.0).then_inc(const_step, 1)
            pool.memset(neghalf[:], -0.5).then_inc(consts, 1)
            pool.wait_ge(const_step, 2)
            pool.affine_select(out=ident[:], in_=ident[:], compare_op=ALU.is_equal, fill=0.0, base=0,
                               pattern=[[-1, P]], channel_multiplier=1).then_inc(consts, 1)
            pool.wait_ge(consts, 3)
            pool.memset(VE[:, :, :, HD:V1], 1.0).then_inc(ve_ones, 1)
            pool.memset(MROW[:].bitcast(F32), 1.0).then_inc(rows_one, 1)
            for b in range(NB):
                t = NC * b
                pool.wait_ge(ln_mv, t + NC)
                pool.tensor_scalar(LV[:, t:t + NC], MV[:, t:t + NC, 1], 1.0, LN_EPS, ALU.mult, ALU.add).then_inc(ln_var, 1)
                pool.wait_ge(ln_var, b + 1)
                pool.tensor_tensor(RS[:, t:t + NC], LV[:, t:t + NC], neghalf[:, 0:NC], ALU.pow).then_inc(ln_rs, 1)
                if b == 0:
                    pool.memset(QZ[:, 0], 0.0).then_inc(qz_zero, 1)
                    pool.wait_ge(mu_in, 16)
                    pool.tensor_tensor(MUQ, MU[:], MU[:], ALU.mult).then_inc(musq, 1)
                if b == 1:
                    pool.memset(QZ[:, 1], 0.0).then_inc(qz_zero, 1)
                if b == 3:
                    pool.memset(GROW[:].bitcast(F32), 1.0).then_inc(rows_one, 1)
                if b == 5:
                    masks()
                if b >= 1:
                    centre(b - 1)
            centre(NB - 1)

            def ev(b):
                if b % GB == 0:
                    pool.wait_ge(rowsT_sb, b // GB + 1)
                if b >= 2:
                    pool.wait_ge(kv_ps, b - 1)
                e = TT[:, 2, H * b:H * b + H].unsqueeze(2).to_broadcast([P, H, HD])
                pool.tensor_tensor(EK[:, b % 2], CX[0][:, b].rearrange("p (h v) -> p h v", h=H), e, ALU.mult).then_inc(ek_sb, 1)

            def head_rs(b):
                u = b % 2
                pool.wait_ge(post_step, 8 * b + 7)
                pool.tensor_scalar(SM[:, u, 7], SM[:, u, 6], 1.0, LN_EPS, ALU.mult, ALU.add).then_inc(gn_var, 1)
                pool.wait_ge(gn_var, b + 1)
                pool.tensor_tensor(SM[:, u, 8], SM[:, u, 7], neghalf[:], ALU.pow).then_inc(gn_rs, 1)

            def affine(b):
                xn = xnb(b)
                pool.wait_ge(xh_sb, NC * (b + 1))
                pool.tensor_tensor(xn, xn, GAM[:].unsqueeze(1).to_broadcast([P, NC, D]), ALU.mult).then_inc(xg_sb, 1)
                pool.wait_ge(xg_sb, b + 1)
                pool.tensor_tensor(xn, xn, BET[:].unsqueeze(1).to_broadcast([P, NC, D]), ALU.add).then_inc(xn_sb, 1)

            def norm(b):
                pool.wait_ge(ss_sb, NC * (b + 1))
                pool.tensor_scalar(SS[:, b, 1], SS[:, b, 0], NORM_FLOOR_SQ, 0.0, ALU.max, ALU.add).then_inc(rn_step, 1)
                pool.wait_ge(rn_step, 2 * b + 1)
                pool.tensor_tensor(SS[:, b, 2], SS[:, b, 1], neghalf[:, 0:NC], ALU.pow).then_inc(rn_step, 1)
                pool.wait_ge(rn_step, 2 * b + 2)
                pool.tensor_tensor(SS[:, b, 3], SS[:, b, 2], SCL[:].to_broadcast([P, NC]), ALU.mult).then_inc(rn_sb, 1)

            def lnrs(b):
                pool.wait_ge(l_var, b + 1)
                pool.tensor_tensor(SS[:, b, 6], SS[:, b, 4], neghalf[:, 0:NC], ALU.pow).then_inc(l_rs, 1)

            ev(0)
            ev(1)
            pool.wait_ge(q_sb, NT)
            pool.wait_ge(vec_in, 16 * NVEC)
            residual(0)
            residual(1)
            for b in range(1, NB + 1):
                if b + 1 < NB:
                    ev(b + 1)
                head_rs(b - 1)
                if 2 <= b:
                    lnrs(b - 2)
                if 3 <= b:
                    affine(b - 3)
                if 4 <= b:
                    norm(b - 4)
                if b + 1 < NB:
                    residual(b + 1)
            pool.memset(HSZ, 0.0).then_inc(hs_zero, 1)
            lnrs(NB - 1)
            affine(NB - 2)
            norm(NB - 3)
            affine(NB - 1)
            norm(NB - 2)
            norm(NB - 1)

        @block.scalar
        def _(act):
            def qk_copy(t):
                act.wait_ge(qk_ps, t + 1)
                act.copy(QKT[:, t].rearrange("p k n -> p (k n)"), PS[:, t % 2, :]).then_inc(qk_sb, 1)
            qk_copy(0)
            qk_copy(1)
            qk_copy(2)
            qk_copy(3)
            act.wait_ge(mu_max, 1)
            act.activation(MUN[:], MUN[:], ACT.Sqrt).then_inc(mu_sqrt, 1)

            def softplus(g):
                act.wait_ge(row_step, 8 * g + 2)
                act.activation(FA[GH:], FA[GH:], ACT.Exp).then_inc(sig_e, 1)
                act.wait_ge(sig_e, g + 1)
                act.activation(FA[GH:], FA[GH:], ACT.Ln, bias=ones[GH:2 * GH, 0:1]).then_inc(sig_l, 1)

            def token_rows(g):
                act.wait_ge(row_step, 8 * g + 8)
                if g == 1:
                    act.wait_ge(rowsT_ps, 1)
                act.activation(ROWS[:, 2, :], G[:, g, 0:P], ACT.Exp, bias=NM[:, g, P - 1:P]).then_inc(tok_rows, 1)
                act.activation(ROWS[:, 3, :], NM[:, g, P:SEQ], ACT.Exp, bias=M[:, g, P - 1:P]).then_inc(tok_rows, 1)
                act.activation(ROWS[:, 0:2, :], CM[:].rearrange("r (c i) -> r c i", c=NC), ACT.Exp,
                               scale=-1.0).then_inc(tok_rows, 1)

            for t in range(4, 12):
                qk_copy(t)
            softplus(0)
            for t in range(12, NT):
                qk_copy(t)
            token_rows(0)

            def decay(b, lo, hi):
                for k in range(4 * b + lo, 4 * b + hi):
                    c, half = (k // 2) % 2, k % 2
                    act.wait_ge(arg_ps, k + 1)
                    if b == 1 and k == 4:
                        act.wait_ge(ve_sb, NT)
                    if b >= 2:
                        act.wait_ge(hd_ps, 2 * (b - 2) + 2)
                    act.activation(DEC[b % 2][:, c, 4 * half:4 * half + 4, :],
                                   PS[:, 4 + k % 2, :].rearrange("p (h i) -> p h i", h=4),
                                   ACT.Exp).then_inc(dec_sb, 1)

            def h0(b):
                act.wait_ge(hd_ps, 2 * b + 1)
                if b >= 2:
                    act.wait_ge(nrm_sb, b - 1)
                act.copy(HB[:, b % 2, 0], PS[:, 6, 0:H * V1].rearrange("p (h v) -> p h v", h=H)).then_inc(h0_sb, 1)

            def squares(b):
                act.wait_ge(h1_sb, b + 1)
                act.wait_ge(h0_sb, b + 1)
                if b >= 1:
                    act.wait_ge(post_step, 8 * (b - 1) + 6)
                act.activation(SQ[:], HB[:, b % 2, :, :, 0:HD], ACT.Square).then_inc(sq_sb, 1)

            def sqn(b):
                act.wait_ge(xn_sb, b + 1)
                for c in range(NC):
                    if b or c:
                        act.wait_ge(ss_sb, NC * b + c)
                    act.activation(JNK[:], xnb(b)[:, c], ACT.Square, accum_out=SS[:, b, 0, c:c + 1]).then_inc(ss_sb, 1)

            def xnt(b):
                act.wait_ge(xnT_ps, b + 1)
                if b == 0:
                    act.wait_ge(ho_ps, 4)
                if b >= 2:
                    act.wait_ge(l_ps, b - 1)
                act.copy(XNT[:, b % 2].rearrange("p k n -> p (k n)"), PS[:, 0, :]).then_inc(xnT_sb, 1)

            def lsb(b):
                act.wait_ge(l_ps, b + 1)
                act.wait_ge(rn_sb, b + 1)
                if b == 0:
                    act.wait_ge(ho_ps, NB)
                if b >= 2:
                    act.wait_ge(lT_ps, b - 1)
                for c in range(NC):
                    act.activation(LSB[:, b % 2, c], PS[:, 1, c * ES:(c + 1) * ES], ACT.Copy,
                                   scale=SS[:, b, 3, c:c + 1]).then_inc(l_sb, 1)

            def ecb(b):
                act.wait_ge(rowmax_sb, b + 1)
                if b >= 2:
                    act.wait_ge(ecT_ps, b - 1)
                for c in range(NC):
                    act.activation(ECB[:, b % 2, c], LSB[:, b % 2, c], ACT.Exp, bias=SS[:, b, 7, c:c + 1],
                                   accum_out=RC[:, b, c:c + 1]).then_inc(ec_sb, 1)

            def edt(b):
                act.wait_ge(colmax_sb, b + 1)
                if b >= 2:
                    act.wait_ge(edT_ps, b - 1)
                for k in range(EC):
                    act.activation(EDT[:, b % 2, k], PS[:, 2, k * SEQ:(k + 1) * SEQ], ACT.Exp,
                                   bias=DM[:, b, k:k + 1], accum_out=DS[:, b, k:k + 1]).then_inc(edt_sb, 1)

            def slot(b):
                act.wait_ge(slot_ps, b + 1)
                if b == 0:
                    act.wait_ge(hd_ps, 2 * NB)
                for k in range(DC):
                    act.copy(SIN[k][:, :, b, :], PS[:, 5, k * ES:(k + 1) * ES].rearrange("p (e s) -> p e s", e=E)).then_inc(slot_sb, 1)

            softplus(1)
            decay(0, 0, 4)
            for b in range(NB):
                if b + 1 < NB:
                    decay(b + 1, 0, 2)
                h0(b)
                if b == 1:
                    token_rows(1)
                if b + 1 < NB:
                    decay(b + 1, 2, 4)
                if b == NB - 1:
                    xnt(0)
                squares(b)
                if 4 <= b:
                    sqn(b - 4)

            for k in range(NB + 5):
                if 3 <= k <= NB + 2:
                    edt(k - 3)
                if 2 <= k <= NB + 1:
                    ecb(k - 2)
                if 1 <= k < NB:
                    xnt(k)
                if 5 <= k:
                    slot(k - 5)
                if 1 <= k <= NB:
                    lsb(k - 1)
                if k == 2:
                    sqn(NB - 4)
                if 4 <= k <= 6:
                    sqn(k + NB - 7)
            for h in range(2):
                act.wait_ge(hpb_sb, h + 1)
                if h == 0:
                    act.wait_ge(hs_zero, 1)
                for q in range(2):
                    rows = slice(q * HID, q * HID + HID)
                    act.activation(HSZ[rows, 4 * h:4 * h + 4, q, :], HPB[rows, 4 * h:4 * h + 4, :],
                                   ACT.Gelu).then_inc(hid_sb, 1)
            for k in range(DC):
                act.wait_ge(so_ps, 2 * k + 2)
                for g in range(2):
                    act.copy(SOT[:, k, :, 4 * g:4 * g + 4, :].rearrange("p b e s -> p e b s"),
                             PS[:, (2 + 4 * k + g) % 8, :].rearrange("p (e b s) -> p e b s", e=4, b=NB)).then_inc(soa_sb, 1)

        @block.tensor
        def _(pe):
            pe.wait_ge(consts, 3)

            def qk_transposes(t):
                b, c = t // NC, t % NC
                pe.wait_ge(q_sb, t + 1)
                pe.wait_ge(c_in[b], 16 * NC)
                if t >= 2:
                    pe.wait_ge(qk_sb, t - 1)
                for k in range(DC):
                    pe.transpose(PS[:, t % 2, k * P:(k + 1) * P], Q[:, t, k * P:(k + 1) * P], ident[:])
                for k in range(DC):
                    tr = pe.transpose(PS[:, t % 2, (DC + k) * P:(DC + k + 1) * P], CX[c][:, b, k * P:(k + 1) * P], ident[:])
                tr.then_inc(qk_ps, 1)

            def gates(b):
                pe.wait_ge(qk_sb, NC * (b + 1))
                if b == GB:
                    pe.wait_ge(mu_max, 1)
                g, w = b // GB, GH - H - H * (b % GB)
                for k in range(4):
                    mm = pe.matmul(PS[0:2 * GH, 2 + g, 0:SEQ], WZ[:, k, w:w + 2 * GH],
                                   QKT[:, NC * b:NC * b + NC, k, :], start=(b % GB == 0 and k == 0),
                                   stop=(b % GB == GB - 1 and k == 3))
                mm.then_inc(gate_ps, 1)

            pe.wait_ge(w_in, 48)
            for k in range(6):
                pe.transpose(PS[:, 3, k * 16:(k + 1) * 16], WW[:, k * P:(k + 1) * P], ident[0:16, 0:16])
            pe.transpose(PS[:, 3, 96:96 + EP], B1L[:], ident[0:EP, 0:EP]).then_inc(wT_ps, 1)
            qk_transposes(0)
            qk_transposes(1)
            qk_transposes(2)
            qk_transposes(3)
            pe.wait_ge(musq, 1)
            pe.wait_ge(b1_sb, 1)
            for k in range(DC):
                mm = pe.matmul(PS[:, 3, 0:ES], ones[:], MUQ[:, k], start=(k == 0), stop=(k == DC - 1))
            mm.then_inc(mu_sum, 1)
            pe.wait_ge(wt_step, 3)
            for b in range(2, NB):
                gates(b - 2)
                qk_transposes(NC * b)
                qk_transposes(NC * b + 1)
            gates(NB - 2)
            gates(NB - 1)

            def args(b, lo, hi):
                if lo == 0:
                    pe.wait_ge(rows_in[b % 2], 64 * (b // 2 + 1))
                for k in range(4 * b + lo, 4 * b + hi):
                    c, half = (k // 2) % 2, k % 2
                    if k >= 2:
                        pe.wait_ge(dec_sb, k - 1)
                    if k == 1:
                        pe.wait_ge(rowsT_sb, 1)
                    if k == 0:
                        pe.wait_ge(late_step, 4)
                    pe.matmul(PS[:, 4 + k % 2, :].rearrange("p (j i) -> p j i", j=4), identr[:],
                              late[:].unsqueeze(1).to_broadcast([P, 4, P]), start=True, stop=False)
                    for j in range(4):
                        h = 4 * half + j
                        mm = pe.matmul(PS[:, 4 + k % 2, j * P:(j + 1) * P], GROW[RB * (b % 2):RB * (b % 2) + 4, h, c * P:(c + 1) * P],
                                       MROW[RB * (b % 2):RB * (b % 2) + 4, h, c * P:(c + 1) * P], start=False, stop=(j == 3))
                    mm.then_inc(arg_ps, 1)

            def scores(b, c, hh):
                if c == 0 and hh == 0:
                    pe.wait_ge(qz_in[b % 2], 16 * HPC * (b // 2 + 1))
                if b == 0 and hh == 0:
                    pe.wait_ge(qk_sb, NT)
                    if c == 1:
                        pe.wait_ge(row_step, 9)
                if b >= 1 and hh == 0:
                    pe.wait_ge(c_sb, NC * (b - 1) + c + 1)
                pe.matmul(PS[:, 2 * c + hh, :], QKT[:, NC * b + c, DC + hh, :],
                          QZ[:, b % 2, :, c, hh, :], start=True, stop=True).then_inc(s_ps, 1)

            def state(b):
                pe.wait_ge(ek_sb, b + 1)
                if b == 0:
                    pe.wait_ge(ve_sb, NT)
                    pe.wait_ge(ve_ones, 1)
                if b >= 1:
                    pe.wait_ge(ho_sb, b)
                for hh in range(H // HPC):
                    mm = pe.matmul(PS[:, 7, hh * HPC * V1:(hh + 1) * HPC * V1],
                                   EK[:, b % 2, hh * HPC:(hh + 1) * HPC, :],
                                   VE[:, NC * b, hh * HPC:(hh + 1) * HPC, :].rearrange("p h v -> p (h v)"),
                                   start=True, stop=True)
                mm.then_inc(kv_ps, 1)

            def apply(b):
                pe.wait_ge(kv_sb, b + 1)
                for hh in range(H // HPC):
                    mm = pe.matmul(PS[:, 7, hh * HPC * V1:(hh + 1) * HPC * V1], QKT[:, NC * b + 1, hh, :],
                                   KVS[:, hh, :], start=True, stop=True)
                mm.then_inc(ho_ps, 1)

            def pv(b, c, half):
                if half == 0:
                    pe.wait_ge(c_sb, NC * b + c + 1)
                    if c == 1:
                        pe.wait_ge(h0_sb, b + 1)
                    elif b >= 1:
                        pe.wait_ge(h1_sb, b)
                        if b == 3:
                            pe.wait_ge(rowsT_sb, 2)
                for h in range(4 * half, 4 * half + 4):
                    mm = pe.matmul(PS[:, 6, h * V1:(h + 1) * V1], DEC[b % 2][:, c, h, :], VE[:, NC * b + c, h, :],
                                   start=True, stop=True)
                if half == 1:
                    mm.then_inc(hd_ps, 1)

            def p_xnT(b):
                pe.wait_ge(xn_sb, b + 1)
                if b >= 1:
                    pe.wait_ge(xnT_sb, b)
                if b == 0:
                    pe.wait_ge(c_sb, NT - 1)
                    pe.wait_ge(mu_step, 2)
                for k in range(DC):
                    for c in range(NC):
                        tr = pe.transpose(PS[:, 0, k * SEQ + c * P:k * SEQ + (c + 1) * P],
                                          xnb(b)[:, c, k * P:(k + 1) * P], ident[:])
                tr.then_inc(xnT_ps, 1)

            def p_l(b):
                pe.wait_ge(xnT_sb, b + 1)
                if b >= 1:
                    pe.wait_ge(l_sb, NC * b)
                for c in range(NC):
                    for k in range(DC):
                        mm = pe.matmul(PS[:, 1, c * ES:(c + 1) * ES], XNT[:, b % 2, k, c * P:(c + 1) * P], MU[:, k],
                                       start=(k == 0), stop=(k == DC - 1))
                mm.then_inc(l_ps, 1)

            def p_lT(b):
                pe.wait_ge(l_sb, NC * (b + 1))
                if b == 0:
                    pe.wait_ge(c_sb, NT)
                if b >= 1:
                    pe.wait_ge(edt_sb, EC * b)
                for k in range(EC):
                    for c in range(NC):
                        tr = pe.transpose(PS[:, 2, k * SEQ + c * P:k * SEQ + (c + 1) * P],
                                          LSB[:, b % 2, c, k * P:(k + 1) * P], ident[:])
                tr.then_inc(lT_ps, 1)

            def p_ecT(b):
                pe.wait_ge(ec_sb, NC * (b + 1))
                if b == 0:
                    pe.wait_ge(dec_sb, 4 * NB)
                if b >= 1:
                    pe.wait_ge(ecT_sb, b)
                for k in range(EC):
                    for c in range(NC):
                        tr = pe.transpose(PS[:, 4, k * SEQ + c * P:k * SEQ + (c + 1) * P],
                                          ECB[:, b % 2, c, k * P:(k + 1) * P], ident[:])
                tr.then_inc(ecT_ps, 1)

            def p_edT(b):
                pe.wait_ge(edt_n, EC * (b + 1))
                if b >= 1:
                    pe.wait_ge(ed_sb, b)
                for c in range(NC):
                    for k in range(EC):
                        tr = pe.transpose(PS[:, 3, c * ES + k * P:c * ES + (k + 1) * P],
                                          EDT[:, b % 2, k, c * P:(c + 1) * P], ident[:])
                tr.then_inc(edT_ps, 1)

            def p_slot(b):
                pe.wait_ge(ed_sb, b + 1)
                if b >= 1:
                    pe.wait_ge(slot_sb, DC * b)
                for k in range(DC):
                    for c in range(NC):
                        mm = pe.matmul(PS[:, 5, k * ES:(k + 1) * ES], xnb(b)[:, c, k * P:(k + 1) * P], ED[:, b % 2, c],
                                       start=(c == 0), stop=(c == NC - 1))
                mm.then_inc(slot_ps, 1)

            def rows_transposes(g):
                pe.wait_ge(tok_rows, 3 * (g + 1))
                c0 = 0 if g == 0 else H * V1
                for i in range(4):
                    tr = pe.transpose(PS[:, 5 + g, c0 + i * GH:c0 + (i + 1) * GH], ROWS[:, i, :], ident[0:GH, 0:GH])
                tr.then_inc(rowsT_ps, 1)

            rows_transposes(0)
            args(0, 0, 4)
            scores(0, 0, 0)
            scores(0, 0, 1)
            scores(0, 1, 0)
            scores(0, 1, 1)
            state(0)
            for b in range(NB):
                more = b + 1 < NB
                for c in range(NC):
                    for half in range(2):
                        if more:
                            args(b + 1, 2 * c + half, 2 * c + half + 1)
                        if b == 2 and c == 1 and half == 1:
                            rows_transposes(1)
                        pv(b, c, half)
                        if more:
                            scores(b + 1, c, half)
                    if c == 0:
                        if not more:
                            p_xnT(0)
                        apply(b)
                if more:
                    state(b + 1)

            for k in range(NB + 5):
                if 4 <= k <= NB + 3:
                    p_edT(k - 4)
                if 3 <= k <= NB + 2:
                    p_ecT(k - 3)
                if 1 <= k < NB:
                    p_xnT(k)
                if 5 <= k:
                    p_slot(k - 5)
                if 1 <= k <= NB:
                    p_l(k - 1)
                if 2 <= k <= NB + 1:
                    p_lT(k - 2)

            pe.wait_ge(slot_sb, DC * NB)
            pe.wait_ge(moe_in, 16 * (DC + 2 + EC * EPC))
            for e in range(E):
                q, p = e % 2, e // 2
                for k in range(DC):
                    mm = pe.matmul(PS[q * HID:(q + 1) * HID, p // 4, (p % 4) * P:(p % 4 + 1) * P], W1[:, k, e, :],
                                   SIN[k][:, e].rearrange("p b s -> p (b s)"), start=(k == 0), stop=(k == DC - 1))
                if e % 8 == 7:
                    mm.then_inc(hid_ps, 1)
            for k in range(DC):
                for p in range(EP):
                    if k == 0 and p % 4 == 0:
                        pe.wait_ge(hid_sb, 2 * (p // 4) + 2)
                    mm = pe.matmul(PS[:, (2 + 4 * k + p // 2) % 8, (p % 2) * 2 * P:(p % 2 + 1) * 2 * P],
                                   W2[:, p, k * P:(k + 1) * P], HSZ[:, p].rearrange("p q n -> p (q n)"),
                                   start=True, stop=True)
                    if p % 4 == 3:
                        mm.then_inc(so_ps, 1)
            pe.wait_ge(soa_sb, 4)
            pe.wait_ge(sov_sb, 4)

            def soT(b):
                if b >= 2:
                    pe.wait_ge(so_sb, b - 1)
                for k in range(EC):
                    for c in range(DC):
                        tr = pe.transpose(PS[:, 2 + b % 2, k * D + c * P:k * D + (c + 1) * P],
                                          SOT[:, c, b, k * EPC:(k + 1) * EPC, :].rearrange("p e s -> p (e s)"), ident[:])
                tr.then_inc(soT_ps, 1)

            def comb(b):
                pe.wait_ge(so_sb, b + 1)
                if b >= 2:
                    pe.wait_ge(y_sb, NC * (b - 1))
                for c in range(NC):
                    for k in range(EC):
                        mm = pe.matmul(PS[:, 4 + b % 2, c * D:(c + 1) * D], ECT[:, b, k, c * P:(c + 1) * P],
                                       SO[:, b % 2, k], start=(k == 0), stop=(k == EC - 1))
                mm.then_inc(y_ps, 1)

            soT(0)
            for b in range(NB):
                if b + 1 < NB:
                    soT(b + 1)
                comb(b)

        @block.vector
        def _(dve):
            def weights():
                dve.wait_ge(wT_ps, 1)
                dve.wait_ge(wz_zero, 1)
                dve.tensor_copy(WTA[:].rearrange("p k g -> p (k g)"), PS[:, 3, 0:96]).then_inc(wt_step, 1)
                dve.tensor_copy(B1[:], PS[:, 3, 96:96 + EP]).then_inc(b1_sb, 1)
                dve.wait_ge(wt_step, 1)
                wz = WZ[:, :, GH - H:GH - H + 2 * GH].rearrange("p k (g r) -> p k g r", g=2)[:, :, :, 0:H]
                wta = WTA[:].rearrange("p k (g h) -> p k g h", g=2)
                dve.tensor_copy(wz[:, 0:2], wta[:, 0:2]).then_inc(wt_step, 1)
                dve.tensor_tensor(wz[:, 2:4], wta[:, 2:4], wta[:, 4:6], ALU.add).then_inc(wt_step, 1)

            def head_means(b):
                dve.wait_ge(c_in[b], 16 * NC)
                for c in range(NC):
                    dve.tensor_reduce(VM[:, NC * b + c], CX[c][:, b].rearrange("p (h v) -> p h v", h=H), AX.X,
                                      ALU.add).then_inc(v_sum, 1)
                dve.wait_ge(v_sum, NC * (b + 1))
                dve.tensor_scalar(VM[:, NC * b:NC * b + NC], VM[:, NC * b:NC * b + NC], 1.0 / HD, None,
                                  ALU.mult).then_inc(v_mean, 1)

            def stats(b):
                dve.wait_ge(x_in[b], 16)
                for t in (NC * b, NC * b + 1):
                    dve.bn_stats(ST[:, t], X[:, t]).then_inc(ln_st, 1)
                for t in (NC * b, NC * b + 1):
                    dve.wait_ge(ln_st, t + 1)
                    dve.bn_aggr(MV[:, t], ST[:, t]).then_inc(ln_mv, 1)

            def norm(b):
                dve.wait_ge(ln_rs, b + 1)
                for t in (NC * b, NC * b + 1):
                    dve.tensor_scalar(Q[:, t], X[:, t], MV[:, t, 0:1], RS[:, t:t + 1],
                                      ALU.subtract, ALU.mult).then_inc(q_sb, 1)
            def gate_rows_a(g):
                st, n = row_step, 8 * g
                dve.wait_ge(gate_ps, GB * (g + 1))
                if g == 0:
                    dve.wait_ge(bias_in, 16 * 2 * GB)
                dve.tensor_scalar(GT[:], PS[0:2 * GH, 2 + g, 0:SEQ], BG[:, 0:1], None, ALU.add).then_inc(st, 1)
                dve.wait_ge(st, n + 1)
                f = GT[GH:]
                dve.scalar_tensor_tensor(out=FA[GH:], in0=f, scalar=-1.0, in1=f, op0=ALU.mult,
                                         op1=ALU.min).then_inc(st, 1)

            def gate_rows_b(g):
                st, n = row_step, 8 * g
                dve.wait_ge(sig_l, g + 1)
                dve.scalar_tensor_tensor(out=LS[:], in0=GT[GH:], scalar=0.0, in1=FA[GH:], op0=ALU.min,
                                         op1=ALU.subtract).then_inc(st, 1)
                dve.wait_ge(st, n + 3)
                dve.tensor_tensor_scan(CS[:], ones[0:GH, 0:1].to_broadcast([GH, SEQ]), LS[:], 0.0,
                                       ALU.mult, ALU.add).then_inc(st, 1)
                dve.wait_ge(st, n + 4)
                dve.tensor_tensor(G[:, g], GT[0:GH], CS[:], ALU.subtract).then_inc(st, 1)
                dve.wait_ge(st, n + 5)
                dve.tensor_tensor_scan(M[:, g], G[:, g], G[:, g], NEG_BIG, ALU.max, ALU.max).then_inc(st, 1)
                dve.wait_ge(st, n + 6)
                dve.tensor_scalar(NM[:, g], M[:, g], -1.0, None, ALU.mult).then_inc(st, 1)
                if g == 1:
                    dve.wait_ge(tok_rows, 3)
                dve.tensor_tensor(CM[:], CS[:], M[:, g], ALU.add).then_inc(st, 1)
                dve.wait_ge(st, n + 8)
                dve.tensor_copy(MHL[:, g, 0], NM[:, g]).then_inc(split, 1)
                dve.tensor_copy(GHL[:, g, 0], G[:, g]).then_inc(split, 1)
                dve.wait_ge(split, 4 * g + 2)
                dve.tensor_tensor(MHL[:, g, 1], NM[:, g], MHL[:, g, 0].bitcast(F32), ALU.subtract).then_inc(split, 1)
                dve.tensor_tensor(GHL[:, g, 1], G[:, g], GHL[:, g, 0].bitcast(F32), ALU.subtract).then_inc(split, 1)

            def token_cols(g):
                dve.wait_ge(rowsT_ps, g + 1)
                c0 = 0 if g == 0 else H * V1
                dve.tensor_copy(TT[:, :, GH * g:GH * g + GH], PS[:, 5 + g, c0:c0 + 4 * GH].rearrange("p (r n) -> p r n", r=4)).then_inc(rowsT_sb, 1)

            def unit_mu():
                dve.wait_ge(mu_sqrt, 1)
                dve.reciprocal(MUN[:], MUN[:]).then_inc(mu_step, 1)
                dve.wait_ge(mu_step, 1)
                dve.tensor_tensor(MU[:], MU[:], MUN[:].unsqueeze(1).to_broadcast([P, DC, ES]), ALU.mult).then_inc(mu_step, 1)

            dve.memset(WZ[:], 0.0).then_inc(wz_zero, 1)
            stats(0)
            stats(1)
            for b in range(NB):
                norm(b)
                if b == 0:
                    weights()
                if b + 2 < NB:
                    stats(b + 2)
                head_means(b)
                if b == 2:
                    dve.wait_ge(mu_sum, 1)
                    dve.tensor_scalar(MUN[:], PS[:, 3, 0:ES], NORM_FLOOR_SQ, None, ALU.max).then_inc(mu_max, 1)
                if b == GB + 1:
                    gate_rows_a(0)
            gate_rows_b(0)
            token_cols(0)
            gate_rows_a(1)
            gate_rows_b(1)

            def kv(b):
                dve.wait_ge(kv_ps, b + 1)
                if b == 0:
                    dve.wait_ge(const_step, 4)
                if b >= 1:
                    dve.wait_ge(ho_ps, b)
                dve.tensor_tensor(KVS[:], PS[:, 7, 0:H * V1].rearrange("p (k v) -> p k v", k=2),
                                  blockmask[:].unsqueeze(1).to_broadcast([P, 2, HPC * V1]), ALU.mult).then_inc(kv_sb, 1)

            def cmul(b, c):
                dve.wait_ge(s_ps, DC * (NC * b + c + 1))
                dve.wait_ge(dec_sb, 4 * b + 2 * c + 2)
                d = DEC[b % 2][:, c].rearrange("p h i -> p (h i)")
                dve.tensor_tensor(d, PS[:, 2 * c:2 * c + 2, :].rearrange("p k n -> p (k n)"),
                                  d, ALU.mult).then_inc(c_sb, 1)

            def ho(b):
                f = TT[:, 3, H * b:H * b + H].unsqueeze(2).to_broadcast([P, H, V1])
                dve.wait_ge(ho_ps, b + 1)
                if b >= 1:
                    dve.wait_ge(h1_sb, b)
                dve.tensor_tensor(HT1[:], PS[:, 7, 0:H * V1].rearrange("p (h v) -> p h v", h=H), f,
                                  ALU.mult).then_inc(ho_sb, 1)

            def h1(b):
                u = b % 2
                dve.wait_ge(hd_ps, 2 * b + 2)
                dve.wait_ge(ho_sb, b + 1)
                dve.tensor_tensor(HB[:, u, 1], PS[:, 6, 0:H * V1].rearrange("p (h v) -> p h v", h=H), HT1[:],
                                  ALU.add).then_inc(h1_sb, 1)

            def sm(b, i):
                return SM[:, b % 2, i].rearrange("p (c h) -> p c h", c=NC)

            def post_a(b):
                u, st, n = b % 2, post_step, 8 * b
                rs = HB[:, u, :, :, HD]
                dve.wait_ge(h1_sb, b + 1)
                dve.wait_ge(h0_sb, b + 1)
                dve.scalar_tensor_tensor(out=sm(b, 1), in0=rs, scalar=-1.0, in1=rs, op0=ALU.mult,
                                         op1=ALU.max).then_inc(st, 1)
                dve.wait_ge(st, n + 1)
                dve.scalar_tensor_tensor(out=sm(b, 2), in0=TT[:, 0:2, H * b:H * b + H], scalar=TAU, in1=sm(b, 1),
                                         op0=ALU.mult, op1=ALU.max).then_inc(st, 1)
                dve.wait_ge(st, n + 2)
                dve.tensor_scalar(SM[:, u, 2], SM[:, u, 2], TAU * 1e-6, None, ALU.add).then_inc(st, 1)
                dve.wait_ge(st, n + 3)
                dve.reciprocal(SM[:, u, 3], SM[:, u, 2]).then_inc(st, 1)
                dve.wait_ge(st, n + 4)
                dve.tensor_tensor(SM[:, u, 4], SM[:, u, 3], SM[:, u, 3], ALU.mult).then_inc(st, 1)
                dve.wait_ge(sq_sb, b + 1)
                dve.tensor_reduce(sm(b, 5), SQ[:], AX.X, ALU.add).then_inc(st, 1)
                dve.wait_ge(st, n + 6)
                dve.scalar_tensor_tensor(out=SM[:, u, 6], in0=SM[:, u, 5], scalar=1.0 / HD, in1=SM[:, u, 4],
                                         op0=ALU.mult, op1=ALU.mult).then_inc(st, 1)

            def post_b(b):
                u, st, n = b % 2, post_step, 8 * b
                dve.wait_ge(gn_rs, b + 1)
                dve.tensor_tensor(SM[:, u, 9], SM[:, u, 8], SM[:, u, 3], ALU.mult).then_inc(st, 1)
                dve.wait_ge(st, n + 8)
                fac = sm(b, 9).unsqueeze(3).to_broadcast([P, NC, H, HD]).rearrange("p c h v -> p (c h) v")
                dve.tensor_tensor(NRM[:, u].rearrange("p c (h v) -> p (c h) v", h=H),
                                  HB[:, u, :, :, 0:HD].rearrange("p c h v -> p (c h) v"), fac, ALU.mult).then_inc(nrm_sb, 1)
                dve.wait_ge(nrm_sb, b + 1)
                dve.tensor_tensor(NRM[:, u], NRM[:, u], GNW[:].unsqueeze(1).to_broadcast([P, NC, D]),
                                  ALU.mult).then_inc(gw_sb, 1)
                dve.wait_ge(gw_sb, b + 1)
                dve.wait_ge(xb_sb, b + 1)
                if b == 0:
                    dve.wait_ge(qk_ps, NT)
                dve.tensor_tensor(Q[:, NC * b:NC * b + NC, :], NRM[:, u], X[:, NC * b:NC * b + NC, :],
                                  ALU.add).then_inc(x1_sb, 1)

            def lstats(b):
                dve.wait_ge(x1_sb, b + 1)
                for t in (NC * b, NC * b + 1):
                    dve.bn_stats(ST[:, t], Q[:, t]).then_inc(l_st, 1)
                for t in (NC * b, NC * b + 1):
                    dve.wait_ge(l_st, t + 1)
                    dve.bn_aggr(MV[:, t], ST[:, t]).then_inc(l_mv, 1)
                dve.wait_ge(l_mv, NC * (b + 1))
                dve.tensor_scalar(SS[:, b, 4], MV[:, NC * b:NC * b + NC, 1], 1.0 + LN_EPS, LN_EPS * LN_EPS,
                                  ALU.mult, ALU.add).then_inc(l_var, 1)

            def lnorm(b):
                dve.wait_ge(l_rs, b + 1)
                if b < 6:
                    dve.wait_ge(ho_ps, b // 2 + 1)
                for c in range(NC):
                    t = NC * b + c
                    dve.tensor_scalar(xnb(b)[:, c], Q[:, t], MV[:, t, 0:1], SS[:, b, 6, c:c + 1],
                                      ALU.subtract, ALU.mult).then_inc(xh_sb, 1)

            def rowmax(b):
                dve.wait_ge(l_sb, NC * (b + 1))
                dve.tensor_reduce(SS[:, b, 7], LSB[:, b % 2], AX.X, ALU.max, negate=True).then_inc(rowmax_sb, 1)

            def colmax(b):
                dve.wait_ge(lT_ps, b + 1)
                dve.tensor_reduce(DM[:, b], PS[:, 2, :].rearrange("p (k n) -> p k n", k=EC), AX.X, ALU.max,
                                  negate=True).then_inc(colmax_sb, 1)

            def dnorm(b):
                dve.wait_ge(edt_sb, EC * (b + 1))
                dve.reciprocal(DR[:, b], DS[:, b]).then_inc(edt_step, 1)
                dve.wait_ge(edt_step, b + 1)
                for k in range(EC):
                    dve.tensor_scalar(EDT[:, b % 2, k], EDT[:, b % 2, k], DR[:, b, k:k + 1], None,
                                      ALU.mult).then_inc(edt_n, 1)

            def ecT(b):
                dve.wait_ge(ecT_ps, b + 1)
                dve.tensor_copy(ECT[:, b].rearrange("p k n -> p (k n)"), PS[:, 4, :]).then_inc(ecT_sb, 1)

            def edc(b):
                dve.wait_ge(edT_ps, b + 1)
                if b >= 2:
                    dve.wait_ge(slot_ps, b - 1)
                dve.tensor_copy(ED[:, b % 2].rearrange("p c e -> p (c e)"), PS[:, 3, :]).then_inc(ed_sb, 1)

            kv(0)
            cmul(0, 0)
            cmul(0, 1)
            for b in range(NB):
                if b == 3:
                    unit_mu()
                if b < NB - 1:
                    ho(b)
                    cmul(b + 1, 0)
                    h1(b)
                if b == 2:
                    token_cols(1)
                if b == NB - 1:
                    rowmax(0)
                if b >= 1:
                    post_b(b - 1)
                if b + 1 < NB:
                    kv(b + 1)
                    cmul(b + 1, 1)
                else:
                    colmax(0)
                    rowmax(1)
                if b == NB - 2:
                    ho(NB - 1)
                post_a(b)
                if b == NB - 2:
                    h1(NB - 1)
                if 2 <= b < NB - 1:
                    lnorm(b - 2)
                if 1 <= b < NB - 1:
                    lstats(b - 1)
            for k in range(3, NB + 5):
                if 4 <= k <= NB + 3:
                    edc(k - 4)
                if 3 <= k <= NB + 2:
                    dnorm(k - 3)
                if 3 <= k <= NB + 2:
                    ecT(k - 3)
                if k <= NB + 1:
                    colmax(k - 2)
                if k <= NB:
                    rowmax(k - 1)
                if k == 4:
                    post_b(NB - 1)
                if 3 <= k <= 4:
                    lnorm(NB - 6 + k)
                    lstats(NB - 5 + k)
                if k == 5:
                    lnorm(NB - 1)
            dve.wait_ge(ec_sb, NT)
            dve.reciprocal(RCI[:], RC[:]).then_inc(rc_sb, 1)

            for h in range(2):
                dve.wait_ge(hid_ps, h + 1)
                dve.tensor_tensor(HPB[:, 4 * h:4 * h + 4, :], PS[:, h, :].rearrange("p (e n) -> p e n", e=4),
                                  B1[:, 4 * h:4 * h + 4].unsqueeze(2).to_broadcast([P, 4, P]), ALU.add).then_inc(hpb_sb, 1)
            for k in range(DC):
                dve.wait_ge(so_ps, 2 * k + 2)
                for g in range(2, 4):
                    dve.tensor_copy(SOT[:, k, :, 4 * g:4 * g + 4, :].rearrange("p b e s -> p e b s"),
                                    PS[:, (2 + 4 * k + g) % 8, :].rearrange("p (e b s) -> p e b s", e=4, b=NB)).then_inc(sov_sb, 1)

            def so(b):
                dve.wait_ge(soT_ps, b + 1)
                if b >= 2:
                    dve.wait_ge(y_ps, b - 1)
                if b == 0:
                    dve.wait_ge(moe_in, 16 * (DC + 2 + EC * EPC))
                dve.tensor_tensor(SO[:, b % 2], PS[:, 2 + b % 2, :].rearrange("p (k d) -> p k d", k=EC), B2R,
                                  ALU.add).then_inc(so_sb, 1)

            def yy(b):
                dve.wait_ge(y_ps, b + 1)
                if b >= 2:
                    dve.wait_ge(y_out[b % 2], 16 * (b // 2))
                if b == 0:
                    dve.wait_ge(rc_sb, 1)
                for c in range(NC):
                    dve.scalar_tensor_tensor(out=Y[:, b % 2, c], in0=PS[:, 4 + b % 2, c * D:(c + 1) * D],
                                             scalar=RCI[:, b, c:c + 1], in1=Q[:, NC * b + c], op0=ALU.mult,
                                             op1=ALU.add).then_inc(y_sb, 1)
            so(0)
            for b in range(NB):
                if b + 1 < NB:
                    so(b + 1)
                yy(b)


_INS = ['x', 'ctx_1024', 'L0_xattn_Wi_w', 'L0_xattn_Wi_b', 'L0_xattn_Wf_w', 'L0_xattn_Wf_b', 'L0_xattn_gn_w',
        'L0_xattn_gn_b', 'L0_ffn_ln_gamma', 'L0_ffn_ln_beta', 'L0_ffn_mu', 'L0_ffn_scale', 'L0_ffn_w1',
        'L0_ffn_b1', 'L0_ffn_w2', 'L0_ffn_b2']


def kernel(**inputs):
    import concourse.bacc as _bacc
    from concourse.bass_utils import run_bass_kernel_spmd as _run

    nc = _bacc.Bacc("TRN2", target_bir_lowering=False, num_devices=1)
    arrays, args = {}, []
    for name in _INS:
        a = np.ascontiguousarray(inputs[name])
        arrays[f"in_{name}"] = a
        args.append(nc.dram_tensor(f"in_{name}", a.shape, mybir.dt.from_np(a.dtype), kind="ExternalInput").ap())
    y = nc.dram_tensor("out_0", tuple(inputs['x'].shape), F32, kind="ExternalOutput").ap()
    xattn_ffn(nc, *args, y)
    r = _run(nc, [arrays], core_ids=[0])
    return r.results[0]["out_0"]
```
